# Optimizing a Trainium2 kernel written in Bass

```python
import numpy as np
import jax
import jax.numpy as jnp

def _softmax(x, axis=-1):
    return jax.nn.softmax(x, axis=axis)

def _gelu(x):
    return jax.nn.gelu(x, approximate=True)

def _silu(x):
    return jax.nn.silu(x)

def _sigmoid(x):
    return jax.nn.sigmoid(x)

def _layernorm(x, axis=-1, eps=1e-05):
    m = jnp.mean(x, axis=axis, keepdims=True)
    v = jnp.var(x, axis=axis, keepdims=True)
    return (x - m) / jnp.sqrt(v + eps)

def _scatter_add(tgt, idx, src, axis=0):
    return tgt.at[idx].add(src)

def _segment_sum(src, seg, n):
    return jax.ops.segment_sum(src, seg, n)
kernel_name = 'mk_decoder_preln_d1_seqx_r4_c86759'

def setup_inputs(seed: int=0):
    np.random.seed(seed)
    _w = jnp.asarray

    def _rec_inputs():
        import jax
        import jax.numpy as jnp
        _rk = jax.random.key(seed)
        x = -0.0005207 + 1.001 * jax.random.normal(jax.random.fold_in(_rk, 1), (64, 256, 256), jnp.float32)
        _lenS = 256 - jax.random.randint(jax.random.fold_in(_rk, 7), (64,), 0, max(1, 256 // 4) + 1, jnp.int32)
        _lenS2 = 120 - jax.random.randint(jax.random.fold_in(_rk, 8), (64,), 0, max(1, 120 // 4) + 1, jnp.int32)
        _ctx_1024P = jax.random.normal(jax.random.fold_in(_rk, 11), (64, 16, 256), jnp.float32)
        _ctx_1024c = jax.random.dirichlet(jax.random.fold_in(_rk, 511), 0.3 * jnp.ones((16,), jnp.float32), (64, 120))
        _ctx_1024t = jnp.einsum('bsk,bkd->bsd', _ctx_1024c, _ctx_1024P)
        _ctx_1024t = _ctx_1024t * jax.lax.rsqrt(jnp.mean(jnp.square(_ctx_1024t)) + 1e-12) * 0.953939
        ctx_1024 = 4.13588e-05 + 0.999923 * (_ctx_1024t + 0.3 * jax.random.normal(jax.random.fold_in(_rk, 611), (64, 120, 256), jnp.float32))
        _validS = jnp.arange(256)[None, :] < _lenS[:, None]
        _validS2 = jnp.arange(120)[None, :] < _lenS2[:, None]
        _causal = jnp.tril(jnp.ones((256, 256), dtype=bool))
        mask_BxSxS2_bk0 = jnp.logical_not(jnp.broadcast_to(_validS2[:, None, :], (64, 256, 120)))
        return (x, ctx_1024, mask_BxSxS2_bk0)
    x, ctx_1024, mask_BxSxS2_bk0 = _rec_inputs()

    def _L0_attn_setup():
        import jax, jax.numpy as jnp
        import numpy as np
        NUM_BITS = 8
        EPS = 1e-08
        N_HEADS = 16

        def fake_quantize(t):
            qmax = 2 ** (NUM_BITS - 1) - 1
            qmin = -2 ** (NUM_BITS - 1)
            max_abs = jnp.max(jnp.abs(jax.lax.stop_gradient(t)))
            scale = jnp.maximum(max_abs / qmax, EPS)
            q = jnp.clip(jnp.round(t / scale), qmin, qmax)
            return q * scale

        def fq_linear(x, W, b):
            return fake_quantize(x) @ fake_quantize(W).T + b
        key = jax.random.key(seed)
        ks = jax.random.split(key, 9)
        B, T, D = (2, 512, 256)
        s = 0.02
        return {'x': jax.random.normal(ks[0], (B, T, D), jnp.float32), 'Wq': jax.random.normal(ks[1], (D, D), jnp.float32) * s, 'bq': jax.random.normal(ks[2], (D,), jnp.float32) * s, 'Wk': jax.random.normal(ks[3], (D, D), jnp.float32) * s, 'bk': jax.random.normal(ks[4], (D,), jnp.float32) * s, 'Wv': jax.random.normal(ks[5], (D, D), jnp.float32) * s, 'bv': jax.random.normal(ks[6], (D,), jnp.float32) * s, 'Wo': jax.random.normal(ks[7], (D, D), jnp.float32) * s, 'bo': jax.random.normal(ks[8], (D,), jnp.float32) * s}
    _L0_attn_all = _L0_attn_setup()
    _L0_attn_in = {k: v for k, v in _L0_attn_all.items() if k in ('Wq', 'bq', 'Wk', 'bk', 'Wv', 'bv', 'Wo', 'bo')}
    del _L0_attn_all

    def _L0_xattn_setup():
        import jax, jax.numpy as jnp
        import numpy as np
        NUM_HEADS = 16

        def softmax1(attn):
            padded = jnp.pad(attn, ((0, 0), (0, 0), (0, 0), (0, 1)))
            return jax.nn.softmax(padded, axis=-1)[..., :-1]
        key = jax.random.key(seed)
        ks = jax.random.split(key, 7)
        B, N, M, C = (2, 256, 1024, 256)
        x = jax.random.normal(ks[0], (B, N, C), dtype=jnp.float32)
        context = jax.random.normal(ks[1], (B, M, C), dtype=jnp.float32)
        mask = jax.random.randint(ks[2], (B, N, M), 0, 2) > 0
        s = 1.0 / np.sqrt(C)
        Wq = jax.random.normal(ks[3], (C, C), dtype=jnp.float32) * s
        Wkv = jax.random.normal(ks[4], (C, 2 * C), dtype=jnp.float32) * s
        Wproj = jax.random.normal(ks[5], (C, C), dtype=jnp.float32) * s
        bproj = jnp.zeros((C,), dtype=jnp.float32)
        return {'x': x, 'context': context, 'mask': mask, 'Wq': Wq, 'Wkv': Wkv, 'Wproj': Wproj, 'bproj': bproj}
    _L0_xattn_all = _L0_xattn_setup()
    _L0_xattn_in = {k: v for k, v in _L0_xattn_all.items() if k in ('Wq', 'Wkv', 'Wproj', 'bproj')}
    del _L0_xattn_all

    def _L0_ffn_setup():
        import jax, jax.numpy as jnp
        import numpy as np
        D_MODEL = 256
        N_HEADS = 16
        HEAD_DIM = D_MODEL // N_HEADS
        FFN_DIM = 1024
        N_EXPERTS = 8
        CAP_FRAC = 0.25
        MOE_TOKEN_DROPOUT = 0.2
        LN_EPS = 1e-05
        B, S = (4, 128)

        def _layer_norm(x, g, b):
            mu = x.mean(-1, keepdims=True)
            var = ((x - mu) ** 2).mean(-1, keepdims=True)
            return (x - mu) * jax.lax.rsqrt(var + LN_EPS) * g + b

        def _self_attention(x, wq, bq, wk, bk, wv, bv, wo, bo):
            b, s, d = x.shape
            q = ((x @ wq + bq) * HEAD_DIM ** (-0.5)).reshape(b, s, N_HEADS, HEAD_DIM)
            k = (x @ wk + bk).reshape(b, s, N_HEADS, HEAD_DIM)
            v = (x @ wv + bv).reshape(b, s, N_HEADS, HEAD_DIM)
            scores = jnp.einsum('bqhd,bkhd->bhqk', q, k)
            p = jax.nn.softmax(scores, axis=-1)
            o = jnp.einsum('bhqk,bkhd->bqhd', p, v).reshape(b, s, d)
            return o @ wo + bo

        def _moe_ffn(x, wr, w1, b1, w2, b2):
            T, D = x.shape
            C = int(np.ceil(CAP_FRAC * T))
            logits = x @ wr
            probs = jax.nn.softmax(logits, axis=-1)
            top1 = jnp.argmax(probs, axis=-1)
            m1 = jax.nn.one_hot(top1, N_EXPERTS, dtype=x.dtype)
            top2 = jnp.argmax(jnp.where(m1 > 0, -jnp.inf, logits), axis=-1)
            m2 = jax.nn.one_hot(top2, N_EXPERTS, dtype=x.dtype)
            loc1 = jnp.cumsum(m1, axis=0) - 1.0
            loc2 = jnp.cumsum(m2, axis=0) - 1.0 + m1.sum(0, keepdims=True)
            m1 = m1 * (loc1 < C)
            m2 = m2 * (loc2 < C)
            t1 = (probs * m1).sum(-1)
            t2 = (probs * m2).sum(-1)
            denom = jnp.maximum(t1 + t2, jnp.finfo(x.dtype).eps)
            t1, t2 = (t1 / denom, t2 / denom)
            tok = jnp.arange(T)
            s1 = loc1[tok, top1].astype(jnp.int32)
            s2 = loc2[tok, top2].astype(jnp.int32)
            v1 = m1[tok, top1] > 0
            v2 = m2[tok, top2] > 0
            s1 = jnp.where(v1, s1, C)
            s2 = jnp.where(v2, s2, C)
            buf = jnp.zeros((N_EXPERTS, C, D), x.dtype)
            buf = buf.at[top1, s1].set(x, mode='drop')
            buf = buf.at[top2, s2].set(x, mode='drop')
            h = jax.nn.relu(jnp.einsum('ecd,edf->ecf', buf, w1) + b1[:, None, :])
            y = (jnp.einsum('ecf,efd->ecd', h, w2) + b2[:, None, :]) * (1.0 - MOE_TOKEN_DROPOUT)
            y1 = y[top1, jnp.minimum(s1, C - 1)]
            y2 = y[top2, jnp.minimum(s2, C - 1)]
            g1 = t1 * v1
            g2 = t2 * v2
            return g1[:, None] * y1 + g2[:, None] * y2
        key = jax.random.key(seed)
        ks = jax.random.split(key, 20)

        def w(k, shape, scale=0.02):
            return jax.random.normal(k, shape, jnp.float32) * scale
        return {'x': jax.random.normal(ks[0], (B, S, D_MODEL), jnp.float32), 'wq': w(ks[1], (D_MODEL, D_MODEL)), 'bq': w(ks[2], (D_MODEL,)), 'wk': w(ks[3], (D_MODEL, D_MODEL)), 'bk': w(ks[4], (D_MODEL,)), 'wv': w(ks[5], (D_MODEL, D_MODEL)), 'bv': w(ks[6], (D_MODEL,)), 'wo': w(ks[7], (D_MODEL, D_MODEL)), 'bo': w(ks[8], (D_MODEL,)), 'ln1_g': 1.0 + w(ks[9], (D_MODEL,)), 'ln1_b': w(ks[10], (D_MODEL,)), 'ln2_g': 1.0 + w(ks[11], (D_MODEL,)), 'ln2_b': w(ks[12], (D_MODEL,)), 'wr': w(ks[13], (D_MODEL, N_EXPERTS)), 'w1': w(ks[14], (N_EXPERTS, D_MODEL, FFN_DIM)), 'b1': w(ks[15], (N_EXPERTS, FFN_DIM)), 'w2': w(ks[16], (N_EXPERTS, FFN_DIM, D_MODEL)), 'b2': w(ks[17], (N_EXPERTS, D_MODEL))}
    _L0_ffn_all = _L0_ffn_setup()
    _L0_ffn_in = {k: v for k, v in _L0_ffn_all.items() if k in ('wq', 'bq', 'wk', 'bk', 'wv', 'bv', 'wo', 'bo', 'ln1_g', 'ln1_b', 'ln2_g', 'ln2_b', 'wr', 'w1', 'b1', 'w2', 'b2')}
    del _L0_ffn_all
    return {'x': x, 'ctx_1024': ctx_1024, 'mask_BxSxS2_bk0': mask_BxSxS2_bk0, 'L0_attn_Wq': _L0_attn_in['Wq'], 'L0_attn_bq': _L0_attn_in['bq'], 'L0_attn_Wk': _L0_attn_in['Wk'], 'L0_attn_bk': _L0_attn_in['bk'], 'L0_attn_Wv': _L0_attn_in['Wv'], 'L0_attn_bv': _L0_attn_in['bv'], 'L0_attn_Wo': _L0_attn_in['Wo'], 'L0_attn_bo': _L0_attn_in['bo'], 'L0_xattn_Wq': _L0_xattn_in['Wq'], 'L0_xattn_Wkv': _L0_xattn_in['Wkv'], 'L0_xattn_Wproj': _L0_xattn_in['Wproj'], 'L0_xattn_bproj': _L0_xattn_in['bproj'], 'L0_ffn_wq': _L0_ffn_in['wq'], 'L0_ffn_bq': _L0_ffn_in['bq'], 'L0_ffn_wk': _L0_ffn_in['wk'], 'L0_ffn_bk': _L0_ffn_in['bk'], 'L0_ffn_wv': _L0_ffn_in['wv'], 'L0_ffn_bv': _L0_ffn_in['bv'], 'L0_ffn_wo': _L0_ffn_in['wo'], 'L0_ffn_bo': _L0_ffn_in['bo'], 'L0_ffn_ln1_g': _L0_ffn_in['ln1_g'], 'L0_ffn_ln1_b': _L0_ffn_in['ln1_b'], 'L0_ffn_ln2_g': _L0_ffn_in['ln2_g'], 'L0_ffn_ln2_b': _L0_ffn_in['ln2_b'], 'L0_ffn_wr': _L0_ffn_in['wr'], 'L0_ffn_w1': _L0_ffn_in['w1'], 'L0_ffn_b1': _L0_ffn_in['b1'], 'L0_ffn_w2': _L0_ffn_in['w2'], 'L0_ffn_b2': _L0_ffn_in['b2']}

def reference(x, ctx_1024, mask_BxSxS2_bk0, L0_attn_Wq, L0_attn_bq, L0_attn_Wk, L0_attn_bk, L0_attn_Wv, L0_attn_bv, L0_attn_Wo, L0_attn_bo, L0_xattn_Wq, L0_xattn_Wkv, L0_xattn_Wproj, L0_xattn_bproj, L0_ffn_wq, L0_ffn_bq, L0_ffn_wk, L0_ffn_bk, L0_ffn_wv, L0_ffn_bv, L0_ffn_wo, L0_ffn_bo, L0_ffn_ln1_g, L0_ffn_ln1_b, L0_ffn_ln2_g, L0_ffn_ln2_b, L0_ffn_wr, L0_ffn_w1, L0_ffn_b1, L0_ffn_w2, L0_ffn_b2):
    import jax
    import jax.numpy as jnp

    def _L0_attn_ref(x, Wq, bq, Wk, bk, Wv, bv, Wo, bo):
        import jax, jax.numpy as jnp
        import numpy as np
        NUM_BITS = 8
        EPS = 1e-08
        N_HEADS = 16

        def fake_quantize(t):
            qmax = 2 ** (NUM_BITS - 1) - 1
            qmin = -2 ** (NUM_BITS - 1)
            max_abs = jnp.max(jnp.abs(jax.lax.stop_gradient(t)))
            scale = jnp.maximum(max_abs / qmax, EPS)
            q = jnp.clip(jnp.round(t / scale), qmin, qmax)
            return q * scale

        def fq_linear(x, W, b):
            return fake_quantize(x) @ fake_quantize(W).T + b
        B, T, D = x.shape
        H = N_HEADS
        Hd = D // H
        scale = Hd ** (-0.5)
        q = fq_linear(x, Wq, bq).reshape(B, T, H, Hd).transpose(0, 2, 1, 3)
        k = fq_linear(x, Wk, bk).reshape(B, T, H, Hd).transpose(0, 2, 1, 3)
        v = fq_linear(x, Wv, bv).reshape(B, T, H, Hd).transpose(0, 2, 1, 3)
        attn = jnp.einsum('bhqd,bhkd->bhqk', q, k) * scale
        causal = jnp.tril(jnp.ones((T, T), dtype=bool))
        attn = jnp.where(causal, attn, -jnp.inf)
        attn = jax.nn.softmax(attn, axis=-1)
        y = jnp.einsum('bhqk,bhkd->bhqd', attn, v)
        y = y.transpose(0, 2, 1, 3).reshape(B, T, D)
        return fq_linear(y, Wo, bo)

    def _L0_xattn_ref(x, context, mask, Wq, Wkv, Wproj, bproj):
        import jax, jax.numpy as jnp
        import numpy as np
        NUM_HEADS = 16

        def softmax1(attn):
            padded = jnp.pad(attn, ((0, 0), (0, 0), (0, 0), (0, 1)))
            return jax.nn.softmax(padded, axis=-1)[..., :-1]
        B, N, C = x.shape
        M = context.shape[1]
        H = NUM_HEADS
        d = C // H
        scale = d ** (-0.5)
        q = (x @ Wq).reshape(B, N, H, d).transpose(0, 2, 1, 3)
        kv = (context @ Wkv).reshape(B, M, 2, H, d)
        k = kv[:, :, 0].transpose(0, 2, 1, 3)
        v = kv[:, :, 1].transpose(0, 2, 1, 3)
        attn = jnp.einsum('bhnd,bhmd->bhnm', q, k) * scale
        neg = -jnp.finfo(attn.dtype).max
        attn = jnp.where(mask[:, None, :, :], neg, attn)
        attn = softmax1(attn)
        out = jnp.einsum('bhnm,bhmd->bhnd', attn, v)
        out = out.transpose(0, 2, 1, 3).reshape(B, N, C)
        return out @ Wproj + bproj

    def _L0_ffn_ref(x, wq, bq, wk, bk, wv, bv, wo, bo, ln1_g, ln1_b, ln2_g, ln2_b, wr, w1, b1, w2, b2):
        import jax, jax.numpy as jnp
        import numpy as np
        D_MODEL = 256
        N_HEADS = 16
        HEAD_DIM = D_MODEL // N_HEADS
        FFN_DIM = 1024
        N_EXPERTS = 8
        CAP_FRAC = 0.25
        MOE_TOKEN_DROPOUT = 0.2
        LN_EPS = 1e-05
        B, S = (4, 128)

        def _layer_norm(x, g, b):
            mu = x.mean(-1, keepdims=True)
            var = ((x - mu) ** 2).mean(-1, keepdims=True)
            return (x - mu) * jax.lax.rsqrt(var + LN_EPS) * g + b

        def _self_attention(x, wq, bq, wk, bk, wv, bv, wo, bo):
            b, s, d = x.shape
            q = ((x @ wq + bq) * HEAD_DIM ** (-0.5)).reshape(b, s, N_HEADS, HEAD_DIM)
            k = (x @ wk + bk).reshape(b, s, N_HEADS, HEAD_DIM)
            v = (x @ wv + bv).reshape(b, s, N_HEADS, HEAD_DIM)
            scores = jnp.einsum('bqhd,bkhd->bhqk', q, k)
            p = jax.nn.softmax(scores, axis=-1)
            o = jnp.einsum('bhqk,bkhd->bqhd', p, v).reshape(b, s, d)
            return o @ wo + bo

        def _moe_ffn(x, wr, w1, b1, w2, b2):
            T, D = x.shape
            C = int(np.ceil(CAP_FRAC * T))
            logits = x @ wr
            probs = jax.nn.softmax(logits, axis=-1)
            top1 = jnp.argmax(probs, axis=-1)
            m1 = jax.nn.one_hot(top1, N_EXPERTS, dtype=x.dtype)
            top2 = jnp.argmax(jnp.where(m1 > 0, -jnp.inf, logits), axis=-1)
            m2 = jax.nn.one_hot(top2, N_EXPERTS, dtype=x.dtype)
            loc1 = jnp.cumsum(m1, axis=0) - 1.0
            loc2 = jnp.cumsum(m2, axis=0) - 1.0 + m1.sum(0, keepdims=True)
            m1 = m1 * (loc1 < C)
            m2 = m2 * (loc2 < C)
            t1 = (probs * m1).sum(-1)
            t2 = (probs * m2).sum(-1)
            denom = jnp.maximum(t1 + t2, jnp.finfo(x.dtype).eps)
            t1, t2 = (t1 / denom, t2 / denom)
            tok = jnp.arange(T)
            s1 = loc1[tok, top1].astype(jnp.int32)
            s2 = loc2[tok, top2].astype(jnp.int32)
            v1 = m1[tok, top1] > 0
            v2 = m2[tok, top2] > 0
            s1 = jnp.where(v1, s1, C)
            s2 = jnp.where(v2, s2, C)
            buf = jnp.zeros((N_EXPERTS, C, D), x.dtype)
            buf = buf.at[top1, s1].set(x, mode='drop')
            buf = buf.at[top2, s2].set(x, mode='drop')
            h = jax.nn.relu(jnp.einsum('ecd,edf->ecf', buf, w1) + b1[:, None, :])
            y = (jnp.einsum('ecf,efd->ecd', h, w2) + b2[:, None, :]) * (1.0 - MOE_TOKEN_DROPOUT)
            y1 = y[top1, jnp.minimum(s1, C - 1)]
            y2 = y[top2, jnp.minimum(s2, C - 1)]
            g1 = t1 * v1
            g2 = t2 * v2
            return g1[:, None] * y1 + g2[:, None] * y2
        h = _layer_norm(x, ln1_g, ln1_b)
        h = _self_attention(h, wq, bq, wk, bk, wv, bv, wo, bo)
        x = x + h
        h = _layer_norm(x, ln2_g, ln2_b)
        b, s, d = h.shape
        moe = _moe_ffn(h.reshape(b * s, d), wr, w1, b1, w2, b2).reshape(b, s, d)
        return x + moe
    x = x + _L0_attn_ref(_layernorm(x, axis=-1), L0_attn_Wq, L0_attn_bq, L0_attn_Wk, L0_attn_bk, L0_attn_Wv, L0_attn_bv, L0_attn_Wo, L0_attn_bo)
    x = x + _L0_xattn_ref(_layernorm(x, axis=-1), ctx_1024, mask_BxSxS2_bk0, L0_xattn_Wq, L0_xattn_Wkv, L0_xattn_Wproj, L0_xattn_bproj)
    x = x + _L0_ffn_ref(_layernorm(x, axis=-1), L0_ffn_wq, L0_ffn_bq, L0_ffn_wk, L0_ffn_bk, L0_ffn_wv, L0_ffn_bv, L0_ffn_wo, L0_ffn_bo, L0_ffn_ln1_g, L0_ffn_ln1_b, L0_ffn_ln2_g, L0_ffn_ln2_b, L0_ffn_wr, L0_ffn_w1, L0_ffn_b1, L0_ffn_w2, L0_ffn_b2)
    return x

_drawn_inputs = setup_inputs


def setup_inputs(seed=0):
    import zlib

    import numpy as np

    out = dict(_drawn_inputs(seed))
    spreads = {'L0_xattn_bproj': (0.0, 0.1)}
    factors = {'L0_attn_Wq': 8.0,
     'L0_attn_bq': 8.0,
     'L0_attn_Wk': 8.0,
     'L0_attn_bk': 64.0,
     'L0_attn_Wv': 3.816,
     'L0_attn_bv': 8.0,
     'L0_attn_Wo': 3.55,
     'L0_attn_bo': 3.046,
     'L0_ffn_wq': 8.0,
     'L0_ffn_bq': 8.0,
     'L0_ffn_wk': 8.0,
     'L0_ffn_bk': 64.0,
     'L0_ffn_bv': 8.0,
     'L0_ffn_bo': 5.012,
     'L0_ffn_ln1_g': 8.0,
     'L0_ffn_ln1_b': 8.0,
     'L0_ffn_ln2_g': 8.0,
     'L0_ffn_ln2_b': 8.0,
     'L0_ffn_b1': 26.159,
     'L0_ffn_b2': 8.0}
    for name, (base, spread) in spreads.items():
        noise = np.random.default_rng([zlib.crc32(name.encode()), seed]).standard_normal(out[name].shape)
        drawn = base * np.exp(spread * noise) if base else spread * noise
        out[name] = jnp.asarray(drawn.astype(out[name].dtype))
    for name, factor in factors.items():
        out[name] = (out[name] * factor).astype(out[name].dtype)
    return out
```

```python
import concourse.bass as bass
from concourse import mybir
from contextlib import ExitStack

F32, BF16, U8, I32 = mybir.dt.float32, mybir.dt.bfloat16, mybir.dt.uint8, mybir.dt.int32
ALU = mybir.AluOpType
ACT = mybir.ActivationFunctionType
AX = mybir.AxisListType
P = 128
MAGIC = 12582912.0
MASKED = -1e30
Q_PARTS = (0, 0, 0, 1, 1, 2)
K_PARTS = (0, 1, 2, 0, 1, 0)


def need(eng, sem, value):
    if isinstance(value, int) and value <= 0:
        return
    eng.wait_ge(sem, value)


def hold(eng, sem, value, passed):
    need(eng, sem, value)
    if not isinstance(value, int):
        eng.sem_inc(passed, 1)


class Chain:

    def __init__(self, eng, sem, start, steps, passed):
        self.eng, self.sem, self.start, self.steps, self.passed, self.done = eng, sem, start, steps, passed, 0

    def step(self, instruction, apart=False):
        self.done += 1
        instruction.then_inc(self.sem, 1)
        if apart:
            hold(self.eng, self.sem, self.start + self.done, self.passed)
        else:
            self.eng.wait_ge(self.sem, self.start + self.done)

    def close(self):
        assert self.done == self.steps, (self.done, self.steps)


def rounds(eng, n):
    yield 0
    with eng.Fori(1, n) as r:
        yield r


def allocators(nc, ctx, prefix):
    def sb(name, shape, dtype=F32):
        return ctx.enter_context(nc.sbuf_tensor(prefix + name, shape, dtype))

    def ps(name, shape, dtype=F32):
        return ctx.enter_context(nc.psum_tensor(prefix + name, shape, dtype))

    sems = []

    def sem(name):
        sems.append(nc.alloc_semaphore(prefix + name))
        return sems[-1]

    def clear():
        nc.clear_and_free_semaphores(sems)
        nc.all_engine_barrier()

    if prefix:
        ctx.callback(clear)

    return sb, ps, sem


def rows(dram, b, n):
    return dram[bass.ds(b * n, n), :].rearrange("(j p) f -> p j f", p=P)


NEWTON = 3
CHAIN_OPS = 2 + 3 * NEWTON


def inverse_root(nc, i, var, y, t):
    v = nc.vector
    if i == 0:
        return v.tensor_scalar(t.bitcast(I32), var.bitcast(I32), 1, None, ALU.logical_shift_right)
    if i == 1:
        return v.tensor_scalar(y.bitcast(I32), t.bitcast(I32), -1.0, float(0x5F3759DF), ALU.mult, ALU.add)
    if i % 3 == 2:
        return v.tensor_tensor(t, y, y, ALU.mult)
    if i % 3 == 0:
        return v.scalar_tensor_tensor(t, t, -0.5, var, ALU.mult, ALU.mult)
    return v.scalar_tensor_tensor(y, t, 1.5, y, ALU.add, ALU.mult)



def setup(nc, C, D, io, slots):
    with ExitStack() as ctx:
        sb, ps, sem = allocators(nc, ctx, "setup_")
        wraw = sb("wraw", [P, 4, 2, 256])
        wq = sb("wq", [P, 4, 2, 256])
        wint = sb("wint", [P, 4, 2, 256], BF16)
        wmax = sb("wmax", [P, 4])
        wmaxall, winv = sb("wmaxall", [P, 4]), sb("winv", [P, 4])
        wt_ps = ps("wt", [P, 2, 256], BF16)
        zeros, zeroed = sb("zeros", [P, D["SLOTS"] * 256 // P // D["CLEARS"]]), sem("zeroed")
        loaded, pooled, wabs, wall, ints, turned, kept, link = (
            sem(n) for n in ("loaded", "pooled", "wabs", "wall", "ints", "turned", "kept", "link"))
        weights = [io["L0_attn_Wq"], io["L0_attn_Wk"], io["L0_attn_Wv"], io["L0_attn_Wo"]]
        loads = []
        for i, w in enumerate(weights):
            loads.append((wraw[:, i, :, :], w.rearrange("(j p) f -> p j f", p=P)))
        for name, dst in C["columns"]:
            loads.append((dst, io[name].rearrange("(m p) -> p m", p=P)))
        for name, dst in C["broadcasts"]:
            loads.append((dst, io[name].rearrange("(o f) -> o f", o=1).partition_broadcast(P)))
        for name, dst in C["matrices"]:
            loads.append((dst, io[name].rearrange("(c p) f -> p c f", p=P)))
        with nc.Block() as block:
            @block.sync
            def _(sp):
                for dst, src in loads:
                    sp.dma_start(dst, src, allow_slow_non_contiguous=True).then_inc(loaded, 16)
                sp.wait_ge(loaded, 16 * len(loads))
                sp.wait_ge(zeroed, 1)
                for r in range(D["CLEARS"]):
                    sp.dma_start(slots.rearrange("(r p n) f -> r p (n f)", p=P, r=D["CLEARS"])[r, :, :], zeros[:, :])\
                        .then_inc(C["slots_cleared"], 16)
                sp.wait_ge(C["slots_cleared"], 16 * D["CLEARS"])

            @block.gpsimd
            def _(pool):
                nc.gpsimd.memset(C["ident_f"][:, :], 0.0).then_inc(pooled, 1)
                nc.gpsimd.memset(C["ident_b"][:, :], 0.0).then_inc(pooled, 1)
                nc.gpsimd.memset(C["causal"][:, :], 0.0).then_inc(pooled, 1)
                nc.gpsimd.memset(C["below"][:, :], 1.0).then_inc(pooled, 1)
                nc.gpsimd.memset(C["ones_b"][:, :], 1.0).then_inc(pooled, 1)
                pool.wait_ge(pooled, 5)
                for m in (C["ident_f"], C["ident_b"]):
                    nc.gpsimd.affine_select(out=m[:, :], in_=m[:, :], compare_op=ALU.not_equal, fill=1.0, base=0,
                                            pattern=[[-1, P]], channel_multiplier=1).then_inc(pooled, 1)
                for h in range(2):
                    half = C["causal"][:, h * P:(h + 1) * P]
                    nc.gpsimd.affine_select(out=half, in_=half, compare_op=ALU.is_ge, fill=MASKED, base=0,
                                            pattern=[[-1, P]], channel_multiplier=1).then_inc(pooled, 1)
                nc.gpsimd.affine_select(out=C["below"][:, :], in_=C["below"][:, :], compare_op=ALU.is_ge, fill=0.0,
                                        base=0, pattern=[[1, P]], channel_multiplier=-1).then_inc(pooled, 1)
                pool.wait_ge(wabs, 4)
                nc.gpsimd.partition_all_reduce(wmaxall[:, :], wmax[:, :], P, bass.bass_isa.ReduceOp.max)\
                    .then_inc(wall, 1)
                pool.wait_ge(wall, 1)

            @block.vector
            def _(dve):
                nc.vector.memset(zeros[:, :], 0.0).then_inc(zeroed, 1)
                chain = Chain(dve, link, 0, 14, C["passed"])
                dve.wait_ge(loaded, 16 * len(loads))
                for i in range(4):
                    nc.vector.tensor_reduce(wmax[:, i:i + 1], wraw[:, i, :, :], AX.XY, ALU.max,
                                            apply_absolute_value=True).then_inc(wabs, 1)
                dve.wait_ge(wall, 1)
                chain.step(nc.vector.tensor_scalar(C["wscale"][:, :], wmaxall[:, :], 1.0 / 127.0, 1e-8, ALU.mult, ALU.max))
                chain.step(nc.vector.reciprocal(winv[:, :], C["wscale"][:, :]))
                for i in range(4):
                    chain.step(nc.vector.tensor_scalar(wq[:, i, :, :], wraw[:, i, :, :], winv[:, i:i + 1], MAGIC,
                                                       ALU.mult, ALU.add))
                    chain.step(nc.vector.tensor_scalar(wq[:, i, :, :], wq[:, i, :, :], MAGIC + 127.0, MAGIC - 128.0,
                                                       ALU.min, ALU.max))
                    nc.vector.tensor_scalar(wint[:, i, :, :], wq[:, i, :, :], MAGIC, None, ALU.subtract)\
                        .then_inc(ints, 1)
                chain.step(nc.vector.tensor_scalar(C["bq_a"][:, :], C["bq_a"][:, :], 0.25, None, ALU.mult))
                chain.step(nc.vector.tensor_scalar(C["bq_f"][:, :], C["bq_f"][:, :], 0.25, None, ALU.mult))
                for kb in C["KS"]:
                    nc.vector.memset(kb[96:98, :, :], -1.0)
                chain.step(nc.vector.memset(C["V"][0][:, :, :, :], 0.0))
                chain.step(nc.vector.memset(C["V"][1][:, :, :, :], 0.0))
                nc.vector.memset(C["V"][0][:, :, :, 16:17], 1.0)
                nc.vector.memset(C["V"][1][:, :, :, 16:17], 1.0).then_inc(kept, 4)
                for i in range(4):
                    dve.wait_ge(turned, i + 1)
                    last = nc.vector.tensor_copy(C["wT"][:, i, :, :], wt_ps[:, :, :])
                    last.then_inc(kept, 1)
                dve.wait_ge(kept, 8)

            @block.tensor
            def _(pe):
                pe.wait_ge(pooled, 10)
                for i in range(4):
                    pe.wait_ge(ints, i + 1)
                    if i:
                        pe.wait_ge(kept, 4 + i)
                    for c in range(2):
                        for j in range(2):
                            last = nc.tensor.transpose(wt_ps[:, c, j * P:(j + 1) * P],
                                                       wint[:, i, j, c * P:(c + 1) * P], C["ident_b"][:, :])
                    last.then_inc(turned, 1)



def first_norm(nc, C, D, io):
    B, NT = D["B"], D["T"] // P
    with ExitStack() as ctx:
        sb, ps, sem = allocators(nc, ctx, "norm_")
        x = [sb(f"x{i}", [P, 2, 256]) for i in range(2)]
        stats, pair = [[sb(f"{n}{i}", [P, 2, w]) for i in range(2)] for n, w in (("stats", 6), ("pair", 2))]
        mean_var, ends = sb("mean_var", [P, NT, 2]), sb("ends", [P, 2, NT])
        root, far = sb("root", [P, 2, NT]), sb("far", [P, 2, NT])
        best, best_all = sb("best", [P, 1]), sb("best_all", [P, 1])
        x_in = [sem(f"x_in{i}") for i in range(2)]
        partial, x_read, link, reduced = (sem(n) for n in ("partial", "x_read", "link", "reduced"))
        with nc.Block() as block:
            @block.sync
            def _(sp):
                for r in rounds(sp, B // 2):
                    for k in range(2):
                        need(sp, x_read, 2 * r + k - 1)
                        sp.dma_start(x[k][:, :, :], rows(io["x"], 2 * r + k, 256)).then_inc(x_in[k], 16)

            @block.vector
            def _(dve):
                v = nc.vector
                for r in rounds(dve, B // 2):
                    for k in range(2):
                        b = 2 * r + k
                        dve.wait_ge(x_in[k], 16 * r + 16)
                        v.bn_stats(stats[k][:, 0, :], x[k][:, 0, :])
                        v.bn_stats(stats[k][:, 1, :], x[k][:, 1, :]).then_inc(partial, 1)
                        v.tensor_reduce(ends[:, 0, bass.ds(2 * b, 2)], x[k][:, :, :], AX.X, ALU.max)
                        v.tensor_reduce(ends[:, 1, bass.ds(2 * b, 2)], x[k][:, :, :], AX.X, ALU.min).then_inc(x_read, 1)
                        hold(dve, partial, 2 * b + 1, C["passed"])
                        v.bn_aggr(pair[k][:, 0, :], stats[k][:, 0, :])
                        v.bn_aggr(pair[k][:, 1, :], stats[k][:, 1, :]).then_inc(partial, 1)
                        dve.wait_ge(partial, 2 * b + 2)
                        v.tensor_copy(mean_var[:, bass.ds(2 * b, 2), :], pair[k][:, :, :]).then_inc(link, 1)
                dve.wait_ge(x_read, B)
                dve.wait_ge(link, B)
                chain = Chain(dve, link, B, 4 + CHAIN_OPS, C["passed"])
                chain.step(v.tensor_copy(C["xmean"][:, :], mean_var[:, :, 0]))
                chain.step(v.tensor_scalar(root[:, 0, :], mean_var[:, :, 1], 1e-5, None, ALU.add))
                for i in range(CHAIN_OPS):
                    chain.step(inverse_root(nc, i, root[:, 0, :], C["xrstd"][:, :], root[:, 1, :]))
                wide = C["xmean"][:, :].unsqueeze(1).broadcast_to([P, 2, NT])
                chain.step(v.tensor_tensor(far[:, :, :], ends[:, :, :], wide, ALU.subtract))
                wide = C["xrstd"][:, :].unsqueeze(1).broadcast_to([P, 2, NT])
                chain.step(v.tensor_tensor(far[:, :, :], far[:, :, :], wide, ALU.mult))
                v.tensor_reduce(best[:, :], far[:, :, :], AX.XY, ALU.max, apply_absolute_value=True).then_inc(reduced, 1)
                chain.close()
                dve.wait_ge(reduced, 2)
                v.tensor_scalar(C["xscale"][:, :], best_all[:, :], 1.0 / 127.0, 1e-8, ALU.mult, ALU.max).then_inc(reduced, 1)
                dve.wait_ge(reduced, 3)
                v.reciprocal(C["xinv"][:, :], C["xscale"][:, :]).then_inc(reduced, 1)
                for i, extra in enumerate((0.25, 1.0, 1.0)):
                    v.tensor_scalar(C["qkv_scale"][:, i:i + 1], C["xscale"][:, :], C["wscale"][:, i:i + 1], extra,
                                    ALU.mult, ALU.mult).then_inc(reduced, 1)
                dve.wait_ge(reduced, 7)

            @block.gpsimd
            def _(pool):
                pool.wait_ge(reduced, 1)
                nc.gpsimd.partition_all_reduce(best_all[:, :], best[:, :], P, bass.bass_isa.ReduceOp.max)\
                    .then_inc(reduced, 1)
                pool.wait_ge(reduced, 2)

H, HD, VW = 16, 16, 32


def attention(nc, C, D, io, scratch, kind):
    B = D["B"]
    KN = 121 if kind == "X" else 256
    KT = 120 if kind == "X" else 256
    KR = KN if kind == "X" else P
    TCOL = {"A": 384, "X": 256, "F": 512}[kind]
    QS, KS, V = C["QS"], C["KS"], C["V"]
    ident_f, ident_b = C["ident_f"], C["ident_b"]
    NEWTON_OPS = ["c%d" % i for i in range(CHAIN_OPS)]

    fill = {
        "A": {0: ["tok0"], 1: ["tok1"], 2: ["v"], 3: ["xT0"], 4: ["xT1"], 5: ["pv0"], 6: ["q"], 7: ["q_rest"], 8: ["k"],
              9: ["pv1", "evac0", "k_rest", "q_store"], 11: ["k_store"], 12: ["norm"], 13: ["pv2"]},
        "X": {0: ["tok0", "v"], 1: ["tok1", "norm"], 2: ["ctxT"], 3: ["aT", "xT"], 4: ["yT"], 5: ["pv0", "q"],
              6: ["proj", "q_rest"], 7: ["wo", "k"], 8: ["stats", "k_rest"], 9: ["pv1", "evac0", "aggr", "q_store"],
              10: ["var", "c0", "k_store"], 11: ["c1", "c2"], 12: ["c3", "c4", "c5"], 13: ["pv2", "c6", "c7"],
              14: ["c8", "c9", "c10"], 15: ["apply"]},
        "F": {0: ["tok0", "h2T0"], 1: ["tok1", "h2T1"], 2: ["v"], 3: ["aT", "route"], 4: ["xT"], 5: ["pv0", "proj", "stats"],
              6: ["q", "ustats"], 7: ["q_rest", "aggr", "uaggr"], 8: ["k", "var", "uvar"],
              9: ["pv1", "evac0", "k_rest", "c0", "q_store"], 10: ["c1", "c2"], 11: ["c3", "c4", "k_store"],
              12: ["c5", "c6"], 13: ["pv2", "c7", "c8"], 14: ["c9", "c10"], 15: ["uapply", "apply"]},
    }[kind]
    STEPS = [("load", 0), ("refetch", 0), ("pv3", 0), ("evac1", 0), ("fetch", 0)]
    head = 0
    for h in range(H):
        STEPS.append(("attend", h))
        STEPS += [(n, 0) for n in fill.get(h, [])]
        for _ in range(2 if 3 <= h < 11 else 0):
            STEPS.append(("maxima", head))
            head += 1
        if h == 11:
            STEPS.append(("rows", 0))
    assert head == H
    LAG = {"load": 1, "v": 1, "maxima": 1, "rows": 1, "attend": 0, "pv0": 0, "pv1": 0, "pv2": 0, "evac0": 0,
           "pv3": -1, "evac1": -1, "refetch": -1, "tok0": -1, "tok1": -1, "aT": -1, "proj": -1,
           "ustats": -1, "uaggr": -1, "uvar": -1, "uapply": -1, "h2T0": -2, "h2T1": -2, "route": -2,
           "ctxT": 2, "xT0": 2, "xT1": 2, "xT": 2, "q": 2, "q_rest": 2, "q_store": 2, "k": 2, "k_rest": 2, "k_store": 2,
           "fetch": 3, "norm": 3, "yT": 3, "wo": 3, "stats": 3, "aggr": 3, "var": 3, "apply": 3}
    LAG.update({c: 3 for c in NEWTON_OPS})
    TURNS = {c: B + 4 if kind == "F" else B for c in NEWTON_OPS}
    UNITS = [n for n, _ in STEPS if n in ("v", "ctxT", "xT0", "xT1", "xT", "q", "k", "yT", "wo", "tok0", "tok1", "aT", "proj",
                                          "h2T0", "h2T1", "route", "rows")]
    NU = len(UNITS)
    assert NU % 2 == 0
    LINKS = {"rows": 3, "norm": {"A": 3, "X": 2, "F": 0}[kind], "stats": 1, "aggr": 1, "var": 1, "ustats": 1, "uaggr": 1,
             "uvar": 1, "tok0": 1, "tok1": 3 if kind == "A" else 1}
    LINKS.update({c: 1 for c in NEWTON_OPS})

    def turns(b, name):
        return b + LAG[name] if not isinstance(b, int) else min(max(b + LAG[name], 0), TURNS.get(name, B))

    def present(b, name):
        return not isinstance(b, int) or 0 <= b + LAG[name] < TURNS.get(name, B)

    def total(b, counts):
        if isinstance(b, int):
            return sum(turns(b, n) * c for n, c in counts)
        return b * sum(c for _, c in counts) + sum(LAG[n] * c for n, c in counts)

    def filling(b, name):
        if isinstance(b, int):
            n = total(b, [(u, 1) for u in UNITS]) + sum(present(b, u) for u in UNITS[:UNITS.index(name)])
            return n % 2, n // 2
        base = sum(LAG[u] for u in UNITS) + UNITS.index(name)
        return base % 2, NU // 2 * b + base // 2

    ORDER = [n for n, _ in STEPS if n in LINKS]

    def linked(b, name):
        return total(b, [(n, LINKS[n]) for n in ORDER]) + \
            sum(LINKS[n] for n in ORDER[:ORDER.index(name)] if present(b, n))

    FIRST, LAST = -3, B - min(LAG[n] for n, _ in STEPS) - 1

    def iterations(eng):
        for b in range(FIRST, 3):
            yield b, b % 2
        with eng.Fori(0, (B - 6) // 2) as r:
            yield 2 * r + 3, 1
            yield 2 * r + 4, 0
        for b in range(B - 3, LAST + 1):
            yield b, b % 2

    def steps(b, par):
        for name, i in STEPS:
            if present(b, name):
                yield name, i, b + LAG[name], (par + LAG[name]) % 2

    with ExitStack() as ctx:
        sb, ps, sem = allocators(nc, ctx, kind + "_")
        work = [ps(f"work{i}", [P, 512]) for i in range(2)]
        score = [ps(f"score{i}", [P, 512]) for i in range(2)]
        scoreT = [ps(f"scoreT{i}", [P, 512]) for i in range(2)]
        outs = ps("outs", [P, 4, 256])
        probs = [sb(f"probs{i}", [P, 4, TCOL]) for i in range(2)]
        outT = sb("outT", [P, 4, 256])
        tok, rec = sb("tok", [P, 2, 256]), sb("rec", [P, 2, H])
        tops, top2 = sb("tops", [P, 3, H]), sb("top2", [P, 2, H])
        top_parts, top_rows = sb("top_parts", [P, 2, 2, H], BF16), sb("top_rows", [32, 256], BF16)
        xdt = BF16 if kind == "A" else F32
        xin, grid = sb("xin", [P, 2, 256]), sb("grid", [P, 2, 256])
        xw, xT = sb("xw", [P, 2, 256], xdt), sb("xT", [P, 2, 256], xdt)
        q_f, k_f, left = sb("q_f", [P, 2, 256]), sb("k_f", [P, 2, 256]), sb("left", [P, 2, 256])
        q_parts, k_parts = sb("q_parts", [P, 3, 2, 256], BF16), sb("k_parts", [P, 3, 2, 256], BF16)
        NR = 6 if kind == "F" else 2
        stats, mean_var, rstd = sb("stats", [P, 2, 6]), sb("mean_var", [P, 2, 2]), sb("rstd", [P, 3, NR])
        aT, xres, zres = sb("aT", [P, 2, 256]), sb("xres", [P, 2, 256]), sb("zres", [P, 2, 256])
        based, summed = sb("based", [P, 2, 256]), sb("summed", [P, 2, 256])
        work_full, work_drained = [[sem(f"{n}{i}") for i in range(2)] for n in ("work_full", "work_drained")]
        (x_in, normed, q_cast0, q_rest, q_cast1, q_split, q_out, k_cast0, k_rest, k_cast1, k_split, k_out, stack_in,
         score_full, score_read, rows_in, scoreT_full, probs_full, pv_done, outs_read, link_v, result_out) = (
             sem(n) for n in ("x_in", "normed", "q_cast0", "q_rest", "q_cast1", "q_split", "q_out", "k_cast0", "k_rest",
                              "k_cast1", "k_split", "k_out", "stack_in", "score_full", "score_read", "rows_in",
                              "scoreT_full", "probs_full", "pv_done", "outs_read", "link_v", "result_out"))
        if kind == "A":
            absmax, best, best_all = sb("absmax", [P, 1]), sb("best", [P, 1]), sb("best_all", [P, 1])
            reduced = sem("reduced")
        if kind == "X":
            yin, yint, yT = sb("yin", [P, 2, 256]), sb("yint", [P, 2, 256], BF16), sb("yT", [P, 2, 256], BF16)
            xb, x1, cin, ctxT = sb("xb", [P, 2, 256]), sb("x1", [P, 2, 256]), sb("cin", [120, 256]), sb("ctxT", [P, 2, 120])
            mraw, mask = sb("mraw", [P, 2, 120], U8), [sb(f"mask{i}", [P, 2, KN], BF16) for i in range(2)]
            zeroed = sem("zeroed")
            y_in, y_ready, ctx_in, mask_in, mask_ready, xb_ready, x1_out, xres_in, based_ready, mask_zero = (
                sem(n) for n in ("y_in", "y_ready", "ctx_in", "mask_in", "mask_ready", "xb_ready", "x1_out", "xres_in",
                                 "based_ready", "mask_zero"))
        if kind == "F":
            z, hn, h2, h2T = sb("z", [P, 2, 256]), sb("hn", [P, 2, 256]), sb("h2", [P, 2, 256]), sb("h2T", [P, 2, 256])
            xu = sb("xu", [P, 2, 256])
            ustats, umean_var, rstd_set = sb("ustats", [P, 2, 6]), sb("umean_var", [P, 2, 2]), sem("rstd_set")
            z_out, zres_in, xres_in, based_ready, hn_ready, xu_ready, h2_ready, h2_out = (
                sem(n) for n in ("z_out", "zres_in", "xres_in", "based_ready", "hn_ready", "xu_ready", "h2_ready", "h2_out"))

        with nc.Block() as block:
            @block.sync
            def _(sp):
                def drained(b, name):
                    if present(b, name):
                        bank, use = filling(b, name)
                        need(sp, work_drained[bank], use + 1)

                if kind == "X":
                    sp.dma_start(cin[:, :], io["ctx"][0:120, :]).then_inc(ctx_in, 16)
                for b, par in iterations(sp):
                    for name, i, g, gp in steps(b, par):
                        if name == "load":
                            hold(sp, q_out, 32 * g + 32, C["passed"])
                            hold(sp, k_out, 32 * g + 32, C["passed"])
                            need(sp, scoreT_full, H * (g - 1))
                            for stack, src, order, n in ((QS, scratch["q"], Q_PARTS, 256), (KS, scratch["k"], K_PARTS, KT)):
                                for blk, part in enumerate(order):
                                    sp.dma_start(stack[gp][16 * blk:16 * blk + 16, :, 0:n],
                                                 src[part, :, 0:n].rearrange("(h d) t -> d h t", d=HD))\
                                        .then_inc(stack_in, 16)
                            if kind == "X":
                                hold(sp, mask_ready, g, C["passed"])
                                sp.dma_start(mraw[:, :, :], rows(io["mask"], g, 256)).then_inc(mask_in, 16)
                        if name == "fetch":
                            need(sp, xb_ready if kind == "X" else normed, g)
                            src = scratch["x2"] if kind == "F" else io["x"]
                            sp.dma_start(xin[:, :, :], rows(src, g, 256)).then_inc(x_in, 16)
                            if kind == "X":
                                need(sp, y_ready, g)
                                sp.dma_start(yin[:, :, :], rows(scratch["y"], g, 256)).then_inc(y_in, 16)
                        if name == "xT" and kind == "X":
                            drained(b, "ctxT")
                            if not isinstance(b, int) or present(b + 1, "xT"):
                                sp.dma_start(cin[:, :], io["ctx"][bass.ds((g + 1) * 120, 120), :]).then_inc(ctx_in, 16)
                        if name == "refetch" and kind == "X":
                            need(sp, x1_out, 16 * g + 16)
                            need(sp, based_ready, g)
                            sp.dma_start(xres[:, :, :], rows(scratch["x1"], g, 256)).then_inc(xres_in, 16)
                        if name == "refetch" and kind == "F":
                            need(sp, z_out, 16 * g + 16)
                            need(sp, based_ready, g)
                            sp.dma_start(zres[:, :, :], rows(scratch["z"], g, 256)).then_inc(zres_in, 16)
                            need(sp, xu_ready, g)
                            sp.dma_start(xres[:, :, :], rows(scratch["x2"], g, 256)).then_inc(xres_in, 16)
                        if name == "tok1" and kind == "A":
                            drained(b, "tok1")
                            sp.dma_start(rows(scratch["y"], g, 256), tok[:, :, :]).then_inc(result_out, 16)
                        if name == "proj" and kind == "X":
                            drained(b, "proj")
                            sp.dma_start(rows(scratch["x2"], g, 256), summed[:, :, :]).then_inc(result_out, 16)
                        if name == "uapply":
                            sp.wait_ge(xu_ready, g + 1)
                            sp.dma_start(rows(scratch["xu"], g, 256), xu[:, :, :]).then_inc(result_out, 16)
                            sp.wait_ge(h2_ready, 2 * g + 2)
                            sp.dma_start(rows(scratch["h2"], g, 256), h2[:, :, :]).then_inc(h2_out, 16)
                        if name == "stats" and kind == "X":
                            drained(b, "wo")
                            sp.dma_start(rows(scratch["x1"], g, 256), x1[:, :, :]).then_inc(x1_out, 16)
                        if name == "apply" and kind == "F":
                            sp.wait_ge(normed, g + 1)
                            sp.dma_start(rows(scratch["z"], g, 256), z[:, :, :]).then_inc(z_out, 16)
                        if name in ("q_store", "k_store"):
                            split, out, parts, n = (q_split, q_out, q_parts, 256) if name[0] == "q" else \
                                (k_split, k_out, k_parts, KT)
                            hold(sp, split, g + 1, C["passed"])
                            need(sp, stack_in, 192 * g)
                            for m in range(2):
                                sp.dma_start(scratch[name[0]][:, m * P:(m + 1) * P, 0:n].rearrange("a p t -> p a t"),
                                             parts[:, :, m, 0:n]).then_inc(out, 16)
                        if name == "rows":
                            drained(b, "rows")
                            for part in range(2):
                                sp.dma_start(QS[gp][96 + part:97 + part, :, :], top_rows[16 * part:16 * part + 16, :])\
                                    .then_inc(rows_in, 16)
                sp.wait_ge(result_out, 16 * B)
                sp.wait_ge(rows_in, 32 * B)
                if kind == "F":
                    sp.wait_ge(h2_out, 16 * B)
                if kind == "X":
                    sp.wait_ge(x1_out, 16 * B)

            @block.tensor
            def _(pe):
                mm = nc.tensor.matmul
                wq, wk, wv, wo = C["w" + kind]
                for b, par in iterations(pe):
                    for name, i, g, gp in steps(b, par):
                        if name in UNITS:
                            bank, use = filling(b, name)
                            W = work[bank]

                        def drained(*names):
                            last = {}
                            for n in names:
                                bk, us = filling(b, n)
                                last[bk] = us
                            for bk, us in last.items():
                                if bk != bank:
                                    need(pe, work_drained[bk], us + 1)

                        if name == "attend":
                            s = scoreT[i % 2]
                            if i == 0:
                                pe.wait_ge(rows_in, 32 * g + 32)
                            need(pe, probs_full, H * g + i - 1)
                            q, k = QS[gp], KS[gp]
                            if kind == "A":
                                for n in range(2):
                                    mm(s[:, n * P:(n + 1) * P], C["causal"][:, 0:P], ident_b[:, :], start=n == 0,
                                       stop=False, skip_group_check=True)
                                mm(s[:, 0:P], k[0:98, i, P:256], q[0:98, i, P:256], start=False, stop=False,
                                   skip_group_check=True)
                                last = mm(s[:, P:384], k[0:98, i, 0:P], q[0:98, i, :], start=False, stop=True,
                                          skip_group_check=True)
                            elif kind == "X":
                                for n in range(2):
                                    mm(s[0:KN, n * P:(n + 1) * P], mask[gp][:, n, :], ident_b[:, :], start=n == 0,
                                       stop=False, skip_group_check=True)
                                last = mm(s[0:KN, 0:256], k[0:98, i, 0:KN], q[0:98, i, :], start=False, stop=True,
                                          skip_group_check=True)
                            else:
                                for n in range(2):
                                    last = mm(s[:, n * 256:(n + 1) * 256], k[0:98, i, n * P:(n + 1) * P], q[0:98, i, :],
                                              start=True, stop=True)
                            last.then_inc(scoreT_full, 1)
                        if name == "maxima":
                            s = score[i % 2]
                            if i == 0:
                                pe.wait_ge(stack_in, 192 * g + 192)
                                if kind == "X":
                                    pe.wait_ge(zeroed, 1)
                                    pe.wait_ge(mask_ready, g + 1)
                            need(pe, score_read, H * g + i - 1)
                            q, k = QS[gp], KS[gp]
                            if kind == "A":
                                mm(s[:, P:384], ident_b[:, :], C["causal"][:, :], start=True, stop=False,
                                   skip_group_check=True)
                                mm(s[:, 0:256], q[0:96, i, P:256], k[0:96, i, :], start=False, stop=False,
                                   skip_group_check=True)
                                last = mm(s[:, 256:384], q[0:96, i, 0:P], k[0:96, i, 0:P], start=False, stop=True,
                                          skip_group_check=True)
                            elif kind == "X":
                                mm(s[:, 0:2 * KN], ident_b[:, :], mask[gp][:, :, :], start=True, stop=False,
                                   skip_group_check=True)
                                for n in range(2):
                                    last = mm(s[:, n * KN:(n + 1) * KN], q[0:96, i, n * P:(n + 1) * P], k[0:96, i, 0:KN],
                                              start=False, stop=n == 1, skip_group_check=True)
                            else:
                                for n in range(2):
                                    last = mm(s[:, n * 256:(n + 1) * 256], q[0:96, i, n * P:(n + 1) * P], k[0:96, i, :],
                                              start=True, stop=True)
                            last.then_inc(score_full, 1)
                        if name[:2] == "pv":
                            m = int(name[2])
                            if m == 0:
                                vb, vu = filling(b - 1, "v")
                                pe.wait_ge(work_drained[vb], vu + 1)
                            pe.wait_ge(probs_full, H * g + 4 * m + 4)
                            need(pe, outs_read, 2 * g + m // 2 - 1)
                            pr = probs[m % 2]
                            if kind == "A":
                                for n in range(2):
                                    for j in range(4):
                                        o = outs[32 * j:32 * j + 32, m, :] if n == 0 else outs[32 * j:32 * j + 32, m, P:256]
                                        x = pr[:, j, P:384] if n == 0 else pr[:, j, 0:P]
                                        last = mm(o, V[gp][:, n, 4 * m + j, :], x, start=n == 0, stop=n == 1,
                                                  skip_group_check=True)
                            elif kind == "X":
                                for j in range(4):
                                    last = mm(outs[32 * j:32 * j + 32, m, :], V[gp][0:KN, 0, 4 * m + j, :], pr[0:KN, j, :],
                                              start=True, stop=True)
                            else:
                                for n in range(2):
                                    for j in range(4):
                                        last = mm(outs[32 * j:32 * j + 32, m, :], V[gp][:, n, 4 * m + j, :],
                                                  pr[:, j, n * 256:(n + 1) * 256], start=n == 0, stop=n == 1,
                                                  skip_group_check=True)
                            last.then_inc(pv_done, 1)
                        if name not in UNITS:
                            continue
                        need(pe, work_drained[bank], use)
                        Wb = W[:, :].bitcast(BF16)
                        if name in ("xT0", "xT1"):
                            j = int(name[2])
                            pe.wait_ge(normed, g + 1)
                            for c in range(2):
                                last = nc.tensor.transpose(Wb[:, c * P:(c + 1) * P], xw[:, j, c * P:(c + 1) * P], ident_b[:, :])
                        elif name == "yT":
                            pe.wait_ge(y_ready, g + 1)
                            for c in range(2):
                                for j in range(2):
                                    last = nc.tensor.transpose(Wb[:, c * 256 + j * P:c * 256 + j * P + P],
                                                               yint[:, j, c * P:(c + 1) * P], ident_b[:, :])
                        elif name == "wo":
                            drained("yT")
                            for j in range(2):
                                for c in range(2):
                                    last = mm(W[:, j * 256:(j + 1) * 256], yT[:, c, j * P:(j + 1) * P], C["wT"][:, 3, c, :],
                                              start=c == 0, stop=c == 1)
                        elif name == "ctxT":
                            pe.wait_ge(ctx_in, 16 * g + 16)
                            for c in range(2):
                                last = nc.tensor.transpose(W[:, c * 120:(c + 1) * 120], cin[:, c * P:(c + 1) * P],
                                                           ident_f[0:120, 0:120])
                        elif name == "xT":
                            pe.wait_ge(normed, g + 1)
                            for c in range(2):
                                for j in range(2):
                                    last = nc.tensor.transpose(W[:, c * 256 + j * P:c * 256 + j * P + P],
                                                               xw[:, j, c * P:(c + 1) * P], ident_f[:, :])
                        elif name in ("q", "k"):
                            src, w, n = (xT, wq, 256) if name == "q" or kind != "X" else (ctxT, wk, KT)
                            w = wq if name == "q" else wk
                            drained("xT1" if kind == "A" else "ctxT" if src is not xT else "xT")
                            for m in range(2):
                                for c in range(2):
                                    last = mm(W[:, m * 256:m * 256 + n], w[:, c, m * P:(m + 1) * P], src[:, c, 0:n],
                                              start=c == 0, stop=c == 1)
                        elif name == "v":
                            if kind == "X":
                                for c in range(2):
                                    last = mm(W[0:120, 0:256], ctxT[:, c, :], wv[:, c, :], start=c == 0, stop=c == 1)
                            else:
                                for j in range(2):
                                    for c in range(2):
                                        last = mm(W[:, j * 256:(j + 1) * 256], xT[:, c, j * P:(j + 1) * P], wv[:, c, :],
                                                  start=c == 0, stop=c == 1)
                        elif name == "rows":
                            pe.wait_ge(link_v, linked(b, "rows") + 3)
                            for j in range(2):
                                last = nc.tensor.transpose(Wb[0:32, j * P:(j + 1) * P],
                                                           top_parts[:, j, :, :].rearrange("p a h -> p (a h)"), ident_b[:, :])
                        elif name in ("tok0", "tok1"):
                            j = int(name[3])
                            pe.wait_ge(outs_read, 2 * g + 2)
                            for m in range(4):
                                last = nc.tensor.transpose(W[:, m * P:(m + 1) * P], outT[:, m, j * P:(j + 1) * P], ident_f[:, :])
                        elif name == "aT":
                            drained("tok0", "tok1")
                            for c in range(2):
                                for j in range(2):
                                    last = nc.tensor.transpose(W[:, c * 256 + j * P:c * 256 + j * P + P],
                                                               tok[:, j, c * P:(c + 1) * P], ident_f[:, :])
                        elif name == "proj":
                            drained("aT")
                            for j in range(2):
                                for c in range(2):
                                    last = mm(W[:, j * 256:(j + 1) * 256], aT[:, c, j * P:(j + 1) * P], wo[:, c, :],
                                              start=c == 0, stop=c == 1)
                        elif name in ("h2T0", "h2T1"):
                            c = int(name[3])
                            pe.wait_ge(h2_ready, 2 * g + 2)
                            for j in range(2):
                                last = nc.tensor.transpose(W[:, j * P:(j + 1) * P], h2[:, j, c * P:(c + 1) * P], ident_f[:, :])
                        elif name == "route":
                            drained("h2T0", "h2T1")
                            for j in range(2):
                                for c in range(2):
                                    last = mm(W[:, j * 8:(j + 1) * 8], h2T[:, c, j * P:(j + 1) * P], C["wr"][:, c, :],
                                              start=c == 0, stop=c == 1)
                        last.then_inc(work_full[bank], 1)

            @block.scalar
            def _(act):
                for b, par in iterations(act):
                    for name, i, g, gp in steps(b, par):
                        if name == "attend":
                            m = i // 4
                            act.wait_ge(scoreT_full, H * g + i + 1)
                            if i % 4 == 0:
                                need(act, pv_done, 4 * g + m - 1)
                            nc.scalar.activation(probs[m % 2][0:KR, i % 4, :], scoreT[i % 2][0:KR, 0:TCOL], ACT.Exp)\
                                .then_inc(probs_full, 1)
                        if name in ("evac0", "evac1"):
                            m = 2 * int(name[4])
                            act.wait_ge(pv_done, 4 * g + m + 2)
                            if name == "evac0" and present(b, "tok1"):
                                bk, us = filling(b, "tok1")
                                act.wait_ge(work_full[bk], us + 1)
                            nc.scalar.activation(outT[:, m:m + 2, :], outs[:, m:m + 2, :], ACT.Copy).then_inc(outs_read, 1)
                        if name not in ("xT0", "xT1", "xT", "yT", "ctxT", "q", "k", "rows", "aT", "h2T0", "h2T1", "q_rest", "k_rest"):
                            continue
                        if name in ("q_rest", "k_rest"):
                            rest, cast, parts, n = (q_rest, q_cast1, q_parts, 256) if name[0] == "q" else \
                                (k_rest, k_cast1, k_parts, KT)
                            act.wait_ge(rest, g + 1)
                            nc.scalar.activation(parts[:, 1, :, 0:n], left[:, :, 0:n], ACT.Copy).then_inc(cast, 1)
                            continue
                        bank, use = filling(b, name)
                        W, Wb = work[bank], work[bank][:, :].bitcast(BF16)

                        def drained(b, name):
                            if present(b, name):
                                bk, us = filling(b, name)
                                need(act, work_drained[bk], us + 1)

                        act.wait_ge(work_full[bank], use + 1)
                        if name in ("xT0", "xT1"):
                            j = int(name[2])
                            drained(b, "v")
                            last = nc.scalar.activation(xT[:, :, j * P:(j + 1) * P],
                                                        Wb[:, 0:256].rearrange("p (c t) -> p c t", c=2), ACT.Copy)
                        elif name == "yT":
                            drained(b - 1, "wo")
                            last = nc.scalar.activation(yT[:, :, :], Wb[:, 0:512].rearrange("p (c t) -> p c t", c=2), ACT.Copy)
                        elif name == "ctxT":
                            drained(b, "v")
                            last = nc.scalar.activation(ctxT[:, :, :], W[:, 0:240].rearrange("p (c t) -> p c t", c=2), ACT.Copy)
                        elif name == "xT" and kind == "X":
                            drained(b, "v")
                            last = nc.scalar.activation(xT[:, :, :], W[:, :].rearrange("p (c t) -> p c t", c=2), ACT.Copy)
                        elif name == "xT":
                            drained(b, "v")
                            for c in range(2):
                                last = nc.scalar.activation(xT[:, c, :], W[:, c * 256:(c + 1) * 256], ACT.Identity,
                                                            bias=C["ln1_b"][:, c:c + 1], scale=C["ln1_g"][:, c:c + 1])
                        elif name in ("q", "k"):
                            dst, split, parts, cast, out = (q_f, q_split, q_parts, q_cast0, q_out) if name == "q" else \
                                (k_f, k_split, k_parts, k_cast0, k_out)
                            n = 256 if name == "q" else KT
                            need(act, split, g)
                            for m in range(2):
                                src = W[:, m * 256:m * 256 + n]
                                if kind == "A":
                                    bias = C["bq_a" if name == "q" else "bk_a"][:, m:m + 1]
                                    scale = C["qkv_scale"][:, 0:1] if name == "q" else C["qkv_scale"][:, 1:2]
                                elif kind == "F":
                                    bias = C["bq_f" if name == "q" else "bk_f"][:, m:m + 1]
                                    scale = 0.25 if name == "q" else 1.0
                                if kind == "X":
                                    last = nc.scalar.activation(dst[:, m, 0:n], src, ACT.Copy, scale=0.25 if name == "q" else 1.0)
                                else:
                                    last = nc.scalar.activation(dst[:, m, 0:n], src, ACT.Identity, bias=bias, scale=scale)
                        elif name == "rows":
                            need(act, rows_in, 32 * g)
                            last = nc.scalar.activation(top_rows[:, :], Wb[0:32, 0:256], ACT.Copy)
                        elif name == "aT":
                            drained(b - 1, "proj")
                            last = nc.scalar.activation(aT[:, :, :], W[:, :].rearrange("p (c t) -> p c t", c=2), ACT.Copy)
                        elif name in ("h2T0", "h2T1"):
                            drained(b - 1, "route")
                            last = nc.scalar.activation(h2T[:, int(name[3]), :], W[:, 0:256], ACT.Copy)
                        last.then_inc(work_drained[bank], 1)
                        if name in ("q", "k"):
                            act.wait_ge(work_drained[bank], use + 1)
                            need(act, out, 32 * g)
                            nc.scalar.activation(parts[:, 0, :, 0:n], dst[:, :, 0:n], ACT.Copy).then_inc(cast, 1)

            @block.vector
            def _(dve):
                if kind == "A":
                    nc.vector.memset(best[:, :], 0.0).then_inc(reduced, 1)
                    dve.wait_ge(reduced, 1)
                if kind == "F":
                    nc.vector.memset(rstd[:, :, :], 1.0).then_inc(rstd_set, 1)
                    dve.wait_ge(rstd_set, 1)
                if kind == "X":
                    for k in KS:
                        nc.vector.memset(k[0:96, :, 120:121], 0.0)
                    nc.vector.memset(V[0][:, :, :, 0:HD], 0.0)
                    nc.vector.memset(V[1][:, :, :, 0:HD], 0.0).then_inc(zeroed, 1)
                    dve.wait_ge(zeroed, 1)
                for b, par in iterations(dve):
                    def drained(b, name):
                        if present(b, name):
                            bk, us = filling(b, name)
                            need(dve, work_drained[bk], us + 1)

                    for name, i, g, gp in steps(b, par):
                        if name in UNITS:
                            bank, use = filling(b, name)
                            W = work[bank]
                        if name in LINKS:
                            chain = Chain(dve, link_v, linked(b, name), LINKS[name], C["passed"])
                        if name == "maxima":
                            dve.wait_ge(score_full, H * g + i + 1)
                            if kind == "A":
                                src, dst = score[i % 2][:, 0:384].rearrange("p (n k) -> p n k", n=3), tops[:, 0:3, i]
                            else:
                                src, dst = score[i % 2][:, 0:2 * KN].rearrange("p (n k) -> p n k", n=2), tops[:, 0:2, i]
                            nc.vector.tensor_reduce(dst, src, AX.X, ALU.max).then_inc(score_read, 1)
                        if name == "rows":
                            dve.wait_ge(score_read, H * g + H)
                            drained(b - 1, "rows")
                            if kind == "A":
                                nc.vector.tensor_copy(top2[:, 0, :], tops[:, 2, :])
                                chain.step(nc.vector.tensor_tensor(top2[:, 1, :], tops[:, 0, :], tops[:, 1, :], ALU.max))
                            else:
                                chain.step(nc.vector.tensor_copy(top2[:, :, :], tops[:, 0:2, :]))
                            chain.step(nc.vector.tensor_copy(top_parts[:, :, 0, :], top2[:, :, :]))
                            chain.step(nc.vector.tensor_tensor(top_parts[:, :, 1, :], top2[:, :, :], top_parts[:, :, 0, :],
                                                               ALU.subtract))
                        if name == "norm" and kind == "A":
                            dve.wait_ge(x_in, 16 * g + 16)
                            drained(b, "xT1")
                            for j in range(2):
                                last = nc.vector.tensor_scalar(grid[:, j, :], xin[:, j, :], C["xmean"][:, bass.ds(2 * g + j, 1)],
                                                               C["xrstd"][:, bass.ds(2 * g + j, 1)], ALU.subtract, ALU.mult)
                            chain.step(last)
                            chain.step(nc.vector.tensor_scalar(grid[:, :, :], grid[:, :, :], C["xinv"][:, :], MAGIC,
                                                               ALU.mult, ALU.add))
                            chain.step(nc.vector.tensor_scalar(grid[:, :, :], grid[:, :, :], MAGIC + 127.0, MAGIC - 128.0,
                                                               ALU.min, ALU.max))
                            nc.vector.tensor_scalar(xw[:, :, :], grid[:, :, :], MAGIC, None, ALU.subtract).then_inc(normed, 1)
                            chain.close()
                        if name == "norm" and kind == "X":
                            dve.wait_ge(y_in, 16 * g + 16)
                            drained(b - 1, "yT")
                            chain.step(nc.vector.tensor_scalar(grid[:, :, :], yin[:, :, :], C["yinv"][:, :], MAGIC,
                                                               ALU.mult, ALU.add))
                            chain.step(nc.vector.tensor_scalar(grid[:, :, :], grid[:, :, :], MAGIC + 127.0, MAGIC - 128.0,
                                                               ALU.min, ALU.max))
                            nc.vector.tensor_scalar(yint[:, :, :], grid[:, :, :], MAGIC, None, ALU.subtract)\
                                .then_inc(y_ready, 1)
                        if name == "wo":
                            dve.wait_ge(xb_ready, g + 1)
                            need(dve, x1_out, 16 * g)
                            dve.wait_ge(work_full[bank], use + 1)
                            nc.vector.scalar_tensor_tensor(x1[:, :, :].rearrange("p j f -> p (j f)"), W[:, :],
                                                           C["yo_scale"][:, :], xb[:, :, :].rearrange("p j f -> p (j f)"),
                                                           ALU.mult, ALU.add).then_inc(work_drained[bank], 1)
                        if name in ("stats", "ustats"):
                            if name == "ustats":
                                pb, pu = filling(b, "proj")
                                dve.wait_ge(work_drained[pb], pu + 1)
                            elif kind == "X":
                                wb, wu = filling(b, "wo")
                                dve.wait_ge(work_drained[wb], wu + 1)
                            else:
                                dve.wait_ge(x_in, 16 * g + 16)
                            x, st = (summed, ustats) if name == "ustats" else (x1 if kind == "X" else xin, stats)
                            nc.vector.bn_stats(st[:, 0, :], x[:, 0, :])
                            nc.vector.bn_stats(st[:, 1, :], x[:, 1, :]).then_inc(link_v, 1)
                        if name in ("aggr", "uaggr"):
                            st, mv = (ustats, umean_var) if name == "uaggr" else (stats, mean_var)
                            hold(dve, link_v, linked(b, name), C["passed"])
                            nc.vector.bn_aggr(mv[:, 0, :], st[:, 0, :])
                            nc.vector.bn_aggr(mv[:, 1, :], st[:, 1, :]).then_inc(link_v, 1)
                        if name in ("var", "uvar"):
                            mv, at = (umean_var, 4) if name == "uvar" else (mean_var, 0)
                            dve.wait_ge(link_v, linked(b, name))
                            if name == "var" and kind == "F":
                                nc.vector.tensor_scalar(rstd[:, 0, 2:4], mv[:, :, 1], 1.0 + 1e-5, 1e-10, ALU.mult, ALU.add)
                            nc.vector.tensor_scalar(rstd[:, 0, at:at + 2], mv[:, :, 1], 1e-5, None, ALU.add).then_inc(link_v, 1)
                        if name in NEWTON_OPS:
                            dve.wait_ge(link_v, linked(b, name))
                            inverse_root(nc, int(name[1:]), rstd[:, 0, :], rstd[:, 1, :], rstd[:, 2, :]).then_inc(link_v, 1)
                        if name == "apply":
                            dve.wait_ge(link_v, linked(b, NEWTON_OPS[-1]) + 1)
                            drained(b, "xT")
                            if kind == "F":
                                need(dve, z_out, 16 * g)
                            x = x1 if kind == "X" else xin
                            for j in range(2):
                                if kind == "F":
                                    nc.vector.tensor_scalar(z[:, j, :], x[:, j, :], mean_var[:, j, 0:1], rstd[:, 1, j:j + 1],
                                                            ALU.subtract, ALU.mult)
                                at = j + 2 if kind == "F" else j
                                last = nc.vector.tensor_scalar(xw[:, j, :], x[:, j, :], mean_var[:, j, 0:1],
                                                               rstd[:, 1, at:at + 1], ALU.subtract, ALU.mult)
                            last.then_inc(normed, 1)
                        if name == "uapply":
                            dve.wait_ge(link_v, linked(b, NEWTON_OPS[-1]) + 1)
                            need(dve, h2_ready, 2 * g)
                            for j in range(2):
                                last = nc.vector.tensor_scalar(hn[:, j, :], summed[:, j, :], umean_var[:, j, 0:1],
                                                               rstd[:, 1, 4 + j:5 + j], ALU.subtract, ALU.mult)
                            last.then_inc(hn_ready, 1)
                        if name == "v":
                            dve.wait_ge(work_full[bank], use + 1)
                            need(dve, pv_done, 4 * (g - 1))
                            n, r = (16, 120) if kind == "X" else (32, P)
                            dst = V[gp][0:r, 0:n // 16, :, 0:HD].rearrange("p a h d -> p (a h) d")
                            src = W[0:r, 0:n * HD].rearrange("p (a d) -> p a d", d=HD)
                            if kind == "X":
                                last = nc.vector.tensor_copy(dst, src)
                            else:
                                scale = C["qkv_scale"][:, 2:3] if kind == "A" else 1.0
                                bias = C["bv" + kind][:, :].rearrange("p (a d) -> p a d", d=HD)
                                last = nc.vector.scalar_tensor_tensor(dst, src, scale, bias, ALU.mult, ALU.add)
                            last.then_inc(work_drained[bank], 1)
                        if name in ("tok0", "tok1"):
                            j = int(name[3])
                            dve.wait_ge(work_full[bank], use + 1)
                            if kind == "A" and j == 0:
                                need(dve, result_out, 16 * g)
                            elif j == 0:
                                drained(b - 1, "aT")
                            v = W[:, :].rearrange("p (h d) -> p h d", d=VW)
                            chain.step(nc.vector.reciprocal(rec[:, j, :], v[:, :, HD]))
                            nc.vector.tensor_tensor(tok[:, j, :].rearrange("p (h d) -> p h d", d=HD), v[:, :, 0:HD],
                                                    rec[:, j, :].unsqueeze(2).broadcast_to([P, H, HD]), ALU.mult)\
                                .then_inc(work_drained[bank], 1)
                            if kind == "A" and j == 1:
                                dve.wait_ge(work_drained[bank], use + 1)
                                chain.step(nc.vector.tensor_reduce(absmax[:, :], tok[:, :, :], AX.XY, ALU.max,
                                                                   apply_absolute_value=True))
                                chain.step(nc.vector.tensor_tensor(best[:, :], best[:, :], absmax[:, :], ALU.max))
                        if name == "proj":
                            dve.wait_ge(work_full[bank], use + 1)
                            dve.wait_ge(based_ready, g + 1)
                            if kind == "X":
                                need(dve, result_out, 16 * g)
                            else:
                                need(dve, xu_ready, g)
                            nc.vector.tensor_tensor(summed[:, :, :].rearrange("p j f -> p (j f)"), W[:, :],
                                                    based[:, :, :].rearrange("p j f -> p (j f)"), ALU.add)\
                                .then_inc(work_drained[bank], 1)
                        if name == "route":
                            dve.wait_ge(work_full[bank], use + 1)
                            nc.vector.tensor_copy(C["logits"][:, bass.ds(2 * g, 2), :],
                                                  W[:, 0:16].rearrange("p (j e) -> p j e", e=8))\
                                .then_inc(work_drained[bank], 1)
                if kind == "A":
                    dve.wait_ge(reduced, 2)
                    nc.vector.tensor_scalar(C["yscale"][:, :], best_all[:, :], 1.0 / 127.0, 1e-8, ALU.mult, ALU.max)\
                        .then_inc(reduced, 1)
                    dve.wait_ge(reduced, 3)
                    nc.vector.reciprocal(C["yinv"][:, :], C["yscale"][:, :]).then_inc(reduced, 1)
                    nc.vector.tensor_tensor(C["yo_scale"][:, :], C["yscale"][:, :], C["wscale"][:, 3:4], ALU.mult)\
                        .then_inc(reduced, 1)
                    dve.wait_ge(reduced, 5)

            @block.gpsimd
            def _(pool):
                if kind == "X":
                    for m in mask:
                        nc.gpsimd.memset(m[:, :, :], 0.0).then_inc(mask_zero, 1)
                    pool.wait_ge(mask_zero, 2)
                for b, par in iterations(pool):
                    for name, i, g, gp in steps(b, par):
                        def drained(b, name):
                            if present(b, name):
                                bk, us = filling(b, name)
                                need(pool, work_drained[bk], us + 1)

                        if name in ("q", "k"):
                            src, parts, cast, rest, n = (q_f, q_parts, q_cast0, q_rest, 256) if name == "q" else \
                                (k_f, k_parts, k_cast0, k_rest, KT)
                            pool.wait_ge(cast, g + 1)
                            nc.gpsimd.tensor_tensor(left[:, :, 0:n], src[:, :, 0:n], parts[:, 0, :, 0:n], ALU.subtract)\
                                .then_inc(rest, 1)
                        if name in ("q_rest", "k_rest"):
                            parts, cast, split, n = (q_parts, q_cast1, q_split, 256) if name[0] == "q" else \
                                (k_parts, k_cast1, k_split, KT)
                            pool.wait_ge(cast, g + 1)
                            nc.gpsimd.tensor_tensor(parts[:, 2, :, 0:n], left[:, :, 0:n], parts[:, 1, :, 0:n], ALU.subtract)\
                                .then_inc(split, 1)
                            pool.wait_ge(split, g + 1)
                        if name == "fetch" and kind == "X":
                            pool.wait_ge(x_in, 16 * g + 16)
                            drained(b - 1, "wo")
                            nc.gpsimd.tensor_tensor(xb[:, :, :], xin[:, :, :], C["bo_a"][:, :, :], ALU.add).then_inc(xb_ready, 1)
                        if name == "load" and kind == "X":
                            pool.wait_ge(mask_in, 16 * g + 16)
                            hold(pool, scoreT_full, H * (g - 1), C["passed"])
                            nc.gpsimd.tensor_scalar(mask[gp][:, :, 0:120], mraw[:, :, :], MASKED, None, ALU.mult)\
                                .then_inc(mask_ready, 1)
                        if name == "refetch" and kind == "X":
                            pool.wait_ge(xres_in, 16 * g + 16)
                            drained(b - 1, "proj")
                            nc.gpsimd.tensor_tensor(based[:, :, :], xres[:, :, :], C["bproj"][:, :, :], ALU.add)\
                                .then_inc(based_ready, 1)
                        if name == "refetch" and kind == "F":
                            pool.wait_ge(zres_in, 16 * g + 16)
                            drained(b - 1, "proj")
                            nc.gpsimd.tensor_tensor(based[:, :, :], zres[:, :, :], C["bo_f"][:, :, :], ALU.add)\
                                .then_inc(based_ready, 1)
                        if name == "uapply":
                            drained(b, "proj")
                            pool.wait_ge(xres_in, 16 * g + 16)
                            need(pool, result_out, 16 * g)
                            nc.gpsimd.tensor_tensor(xu[:, :, :], summed[:, :, :], xres[:, :, :], ALU.add).then_inc(xu_ready, 1)
                            pool.wait_ge(hn_ready, g + 1)
                            need(pool, h2_out, 16 * g)
                            drained(b, "h2T1")
                            nc.gpsimd.tensor_tensor(h2[:, :, :], hn[:, :, :], C["ln2_g"][:, :, :], ALU.mult)\
                                .then_inc(h2_ready, 1)
                            pool.wait_ge(h2_ready, 2 * g + 1)
                            nc.gpsimd.tensor_tensor(h2[:, :, :], h2[:, :, :], C["ln2_b"][:, :, :], ALU.add)\
                                .then_inc(h2_ready, 1)
                            pool.wait_ge(h2_ready, 2 * g + 2)
                if kind == "A":
                    pool.wait_ge(link_v, linked(LAST + 1, ORDER[0]))
                    nc.gpsimd.partition_all_reduce(best_all[:, :], best[:, :], P, bass.bass_isa.ReduceOp.max)\
                        .then_inc(reduced, 1)
                    pool.wait_ge(reduced, 2)



NE = 8


def route(nc, C, D, io):
    NT, CAP = D["T"] // P, D["CAP"]
    with ExitStack() as ctx:
        sb, ps, sem = allocators(nc, ctx, "route_")
        L = C["logits"]
        first, hit, other, spread = (sb(n, [P, NT, NE]) for n in ("first", "hit", "other", "spread"))
        one = [sb(f"one{i}", [P, NT, NE]) for i in range(2)]
        one_b = [sb(f"one_b{i}", [P, NT, NE], BF16) for i in range(2)]
        loc = sb("loc", [P, NT, NE])
        run = [sb(f"run{i}", [P, NT, NE]) for i in range(2)]
        down, ones = sb("down", [P, NE]), sb("ones", [P, NT])
        top = [sb(f"top{i}", [P, NT]) for i in range(2)]
        rank = [sb(f"rank{i}", [P, NT]) for i in range(2)]
        pos = [sb(f"pos{i}", [P, NT]) for i in range(2)]
        kept = [sb(f"kept{i}", [P, NT]) for i in range(2)]
        prob = [sb(f"prob{i}", [P, NT]) for i in range(2)]
        base, slot, total, den = sb("base", [P, NT]), sb("slot", [P, NT]), sb("total", [P, NT]), sb("den", [P, NT])
        b1_rows = sb("b1_rows", [NE * 8, P])
        HALF = max(NT * NE // 512, 1)
        W = NT * NE // HALF
        inside = [ps(f"inside{i}", [P, HALF, 512]) for i in range(2)]
        whole = [ps(f"whole{i}", [P, HALF, 512]) for i in range(2)]
        link, hot, counted, spread_in, exped, b1_in, b1_turned = (
            sem(n) for n in ("link", "hot", "counted", "spread_in", "exped", "b1_in", "b1_turned"))

        def flat(t):
            return t[:, :, :].rearrange("p n e -> p (n e)")

        def cols(t):
            return t[:, :, 0:W] if HALF > 1 else t[:, 0, 0:W]

        def halves(t):
            return flat(t).rearrange("p (a w) -> p a w", a=HALF) if HALF > 1 else flat(t)

        def wide(t):
            return t[:, :].unsqueeze(2).broadcast_to([P, NT, NE])

        with nc.Block() as block:
            @block.sync
            def _(sp):
                sp.dma_start(b1_rows[:, :], io["L0_ffn_b1"].rearrange("e (f p) -> (e f) p", p=P)).then_inc(b1_in, 16)

            @block.tensor
            def _(pe):
                for i in range(2):
                    pe.wait_ge(hot, i + 1)
                    for a in range(HALF):
                        m = flat(one_b[i])[:, a * W:(a + 1) * W]
                        nc.tensor.matmul(inside[i][:, a, 0:W], C["below"][:, :], m, start=True, stop=True)
                        last = nc.tensor.matmul(whole[i][:, a, 0:W], C["ones_b"][:, :], m, start=True, stop=True)
                    last.then_inc(counted, 1)
                pe.wait_ge(counted, 3)
                pe.wait_ge(b1_in, 16)
                nc.tensor.transpose(inside[0][:, 0, 0:NE * 8], b1_rows[:, :], C["ident_f"][0:NE * 8, 0:NE * 8])\
                    .then_inc(b1_turned, 1)

            @block.scalar
            def _(act):
                act.wait_ge(spread_in, 1)
                nc.scalar.activation(flat(other), flat(spread), ACT.Exp)
                nc.scalar.activation(prob[1][:, :], total[:, :], ACT.Exp).then_inc(exped, 1)

            @block.vector
            def _(dve):
                chain = Chain(dve, link, 0, None, C["passed"])
                v = nc.vector
                for e in range(NE):
                    v.memset(down[:, e:e + 1], float(NE - e))
                v.memset(ones[:, :], 1.0)
                chain.step(v.tensor_copy(flat(first), flat(L)))
                down3 = down[:, :].unsqueeze(1).broadcast_to([P, NT, NE])
                for i in range(2):
                    chain.step(v.tensor_reduce(top[i][:, :], first[:, :, :], AX.X, ALU.max))
                    chain.step(v.tensor_tensor(hit[:, :, :], first[:, :, :], wide(top[i]), ALU.is_equal))
                    chain.step(v.tensor_tensor(hit[:, :, :], hit[:, :, :], down3, ALU.mult))
                    chain.step(v.tensor_reduce(rank[i][:, :], hit[:, :, :], AX.X, ALU.max))
                    chain.step(v.tensor_tensor(one[i][:, :, :], wide(rank[i]), down3, ALU.is_equal))
                    v.tensor_copy(flat(one_b[i]), flat(one[i])).then_inc(hot, 1)
                    if i == 0:
                        chain.step(v.scalar_tensor_tensor(flat(first), flat(one[0]), -3e38, flat(first), ALU.mult, ALU.add))
                v.tensor_tensor(spread[:, :, :], L[:, :, :], wide(top[0]), ALU.subtract)
                v.tensor_tensor(total[:, :], top[1][:, :], top[0][:, :], ALU.subtract).then_inc(spread_in, 1)
                dve.wait_ge(exped, 1)
                chain.step(v.tensor_reduce(den[:, :], other[:, :, :], AX.X, ALU.add))
                chain.step(v.reciprocal(prob[0][:, :], den[:, :]))
                chain.step(v.tensor_tensor(prob[1][:, :], prob[1][:, :], prob[0][:, :], ALU.mult))
                for i in range(2):
                    dve.wait_ge(counted, i + 1)
                    chain.step(v.tensor_copy(halves(hit), cols(whole[i])))
                    for e in range(NE):
                        last = v.tensor_tensor_scan(run[i][:, :, e], ones[:, :], hit[:, :, e], 0.0, ALU.mult, ALU.add)
                    chain.step(last)
                    chain.step(v.tensor_tensor(flat(loc), flat(run[i]), flat(hit), ALU.subtract))
                    chain.step(v.tensor_tensor(halves(loc), cols(inside[i]), halves(loc), ALU.add))
                    if i == 1:
                        every = run[0][:, NT - 1:NT, :].broadcast_to([P, NT, NE])
                        chain.step(v.tensor_tensor(loc[:, :, :], loc[:, :, :], every, ALU.add))
                    chain.step(v.tensor_tensor(flat(loc), flat(loc), flat(one[i]), ALU.mult))
                    chain.step(v.tensor_reduce(pos[i][:, :], loc[:, :, :], AX.X, ALU.add))
                    chain.step(v.tensor_scalar(pos[i][:, :], pos[i][:, :], -1.0, None, ALU.add))
                    chain.step(v.tensor_scalar(kept[i][:, :], pos[i][:, :], float(CAP), None, ALU.is_lt))
                    chain.step(v.tensor_scalar(base[:, :], rank[i][:, :], -float(CAP), float(NE * CAP), ALU.mult, ALU.add))
                    chain.step(v.tensor_scalar(slot[:, :], pos[i][:, :], float(CAP - 1), None, ALU.min))
                    chain.step(v.tensor_tensor(slot[:, :], slot[:, :], base[:, :], ALU.add))
                    chain.step(v.tensor_copy(C["gather"][i][:, 0:NT], slot[:, :]))
                    v.memset(C["gather"][i][:, NT:NT + 4], 0)
                    chain.step(v.tensor_scalar(base[:, :], kept[i][:, :], -float(4 * NE * CAP), float(4 * NE * CAP),
                                               ALU.mult, ALU.add))
                    chain.step(v.tensor_tensor(slot[:, :], slot[:, :], base[:, :], ALU.add))
                    chain.step(v.tensor_copy(C["scatter"][i][:, :], slot[:, :]))
                    chain.step(v.tensor_tensor(prob[i][:, :], prob[i][:, :], kept[i][:, :], ALU.mult))
                chain.step(v.tensor_tensor(den[:, :], prob[0][:, :], prob[1][:, :], ALU.add))
                chain.step(v.tensor_scalar(den[:, :], den[:, :], 1.1920928955078125e-07, None, ALU.max))
                chain.step(v.reciprocal(total[:, :], den[:, :]))
                for i in range(2):
                    chain.step(v.tensor_tensor(base[:, :], prob[i][:, :], total[:, :], ALU.mult))
                    chain.step(v.tensor_tensor(C["gate"][i][:, :], base[:, :], kept[i][:, :], ALU.mult))
                v.memset(ones[:, 0:1], 0.0).then_inc(counted, 1)
                dve.wait_ge(b1_turned, 1)
                chain.step(v.tensor_copy(C["b1"][:, :], inside[0][:, 0, 0:NE * 8]))



def dispatch(nc, C, D, io, scratch):
    NT, CAP = D["T"] // P, D["CAP"]
    R = 4
    with ExitStack() as ctx:
        sb, ps, sem = allocators(nc, ctx, "disp_")
        h2 = [sb(f"h2{i}", [P, 256]) for i in range(R)]
        index = [sb(f"index{i}", [P, 2], I32) for i in range(R)]
        h2_in = [sem(f"h2_in{i}") for i in range(R)]
        sent = [sem(f"sent{i}") for i in range(R)]
        index_ready = sem("index_ready")
        with nc.Block() as block:
            @block.sync
            def _(sp):
                for r in rounds(sp, NT // R):
                    for k in range(R):
                        need(sp, sent[k], 32 * r)
                        sp.dma_start(h2[k][:, :], scratch["h2"][bass.ds((R * r + k) * P, P), :]).then_inc(h2_in[k], 16)

            @block.vector
            def _(dve):
                for r in rounds(dve, NT // R):
                    for k in range(R):
                        need(dve, sent[k], 32 * r)
                        for i in range(2):
                            last = nc.vector.tensor_copy(index[k][:, i:i + 1], C["scatter"][i][:, bass.ds(R * r + k, 1)])
                        last.then_inc(index_ready, 1)

            @block.gpsimd
            def _(pool):
                pool.wait_ge(C["slots_cleared"], 16 * D["CLEARS"])
                for r in rounds(pool, NT // R):
                    for k in range(R):
                        hold(pool, index_ready, R * r + k + 1, C["passed"])
                        hold(pool, h2_in[k], 16 * r + 16, C["passed"])
                        for i in range(2):
                            nc.gpsimd.indirect_dma_start(
                                scratch["slots"], bass.IndirectOffsetOnAxis(index[k][:, i:i + 1], 0), h2[k][:, :], None,
                                bounds_check=NE * CAP - 1, oob_is_err=False).then_inc(sent[k], 16)
                for k in range(R):
                    pool.wait_ge(sent[k], 32 * (NT // R))



def experts(nc, C, D, io, scratch):
    CAP = D["CAP"]
    NS = 512
    NC = CAP // NS
    NF = 1024 // P
    with ExitStack() as ctx:
        sb, ps, sem = allocators(nc, ctx, "exp_")
        w1 = [sb(f"w1{i}", [P, 2, 1024]) for i in range(2)]
        w2 = [sb(f"w2{i}", [P, NF, 256]) for i in range(2)]
        b1 = [sb(f"b1{i}", [P, NF]) for i in range(2)]
        b2 = [sb(f"b2{i}", [P, 256]) for i in range(2)]
        b2s = [sb(f"b2s{i}", [P, 2, 256]) for i in range(2)]
        x = [sb(f"x{i}", [P, 4, 256]) for i in range(2)]
        xT = [sb(f"xT{i}", [P, 2, NS]) for i in range(2)]
        hT = [sb(f"hT{i}", [P, NF, NS]) for i in range(2)]
        y = [sb(f"y{i}", [P, 4, 256]) for i in range(2)]
        turn = [ps(f"turn{i}", [P, NS]) for i in range(2)]
        hid = [ps(f"hid{i}", [P, NS]) for i in range(2)]
        res = [ps(f"res{i}", [P, 2, 256]) for i in range(2)]
        w_in = [sem(f"w_in{i}") for i in range(2)]
        x_in = [sem(f"x_in{i}") for i in range(2)]
        y_out = [sem(f"y_out{i}") for i in range(2)]
        (turned, xT_ready, hid_full, hid_read, res_full, res_read, biases) = (sem(n) for n in (
            "turned", "xT_ready", "hid_full", "hid_read", "res_full", "res_read", "biases"))

        def chunks(r):
            for k in range(2):
                for c in range(NC):
                    j = k * NC + c
                    yield 2 * r + k, k, c, j % 2, 2 * NC * r + j

        with nc.Block() as block:
            @block.sync
            def _(sp):
                def weights(e, k):
                    for dst, src in ((w1[k][:, :, :], io["L0_ffn_w1"][bass.ds(e * 256, 256), :].rearrange("(c p) f -> p c f", p=P)),
                                     (w2[k][:, :, :], io["L0_ffn_w2"][bass.ds(e * 1024, 1024), :].rearrange("(f p) n -> p f n", p=P)),
                                     (b2[k][:, :], io["L0_ffn_b2"][bass.ds(e, 1), :].partition_broadcast(P))):
                        sp.dma_start(dst, src).then_inc(w_in[k], 16)

                def rows_in(k, n):
                    sp.dma_start(x[k][:, :, :], scratch["slots"][bass.ds(n * NS, NS), :].rearrange("(j p) f -> p j f", p=P))\
                        .then_inc(x_in[k], 16)

                weights(0, 0)
                rows_in(0, 0)
                weights(1, 1)

                def round_of(r, last):
                    for e, k, c, par, n in chunks(r):
                        if not last or n + 1 < NE * NC:
                            need(sp, turned, 2 * n)
                            rows_in(1 - par, n + 1)
                        sp.wait_ge(res_read, 2 * n + 2)
                        sp.dma_start(scratch["yslots"][bass.ds(n * NS, NS), :].rearrange("(j p) f -> p j f", p=P),
                                     y[par][:, :, :]).then_inc(y_out[par], 16)
                        if c == NC - 1 and not last:
                            weights(e + 2, k)

                for r in rounds(sp, NE // 2 - 1):
                    round_of(r, False)
                round_of(NE // 2 - 1, True)
                for k in range(2):
                    sp.wait_ge(y_out[k], 16 * (NE * NC // 2))
                    sp.wait_ge(w_in[k], 48 * (NE // 2))

            @block.tensor
            def _(pe):
                for r in rounds(pe, NE // 2):
                    for e, k, c, par, n in chunks(r):
                        pe.wait_ge(x_in[par], 8 * (n - par) + 16)
                        for a in range(2):
                            need(pe, xT_ready, 2 * n)
                            for j in range(4):
                                last = nc.tensor.transpose(turn[a][:, j * P:(j + 1) * P], x[par][:, j, a * P:(a + 1) * P],
                                                           C["ident_f"][:, :])
                            last.then_inc(turned, 1)
                        if c == 0:
                            pe.wait_ge(w_in[k], 48 * r + 48)
                        pe.wait_ge(xT_ready, 2 * n + 2)
                        for f in range(NF):
                            m = NF * n + f
                            if k or c or f >= 2:
                                need(pe, hid_read, m - 1)
                            h = hid[f % 2]
                            for a in range(2):
                                last = nc.tensor.matmul(h[:, :], w1[k][:, a, f * P:(f + 1) * P], xT[par][:, a, :],
                                                        start=a == 0, stop=a == 1)
                            last.then_inc(hid_full, 1)
                        pe.wait_ge(hid_read, NF * n + NF)
                        for t in range(2):
                            need(pe, res_read, 2 * n)
                            for s in range(2):
                                for f in range(NF):
                                    last = nc.tensor.matmul(res[t][:, s, :], hT[par][:, f, (2 * t + s) * P:(2 * t + s + 1) * P],
                                                            w2[k][:, f, :], start=f == 0, stop=f == NF - 1)
                            last.then_inc(res_full, 1)

            @block.scalar
            def _(act):
                for r in rounds(act, NE // 2):
                    for e, k, c, par, n in chunks(r):
                        if c == 0:
                            act.wait_ge(biases, 2 * e + 2)
                        for f in range(NF):
                            act.wait_ge(hid_full, NF * n + f + 1)
                            nc.scalar.activation(hT[par][:, f, :], hid[f % 2][:, :], ACT.Relu, bias=b1[k][:, f:f + 1])\
                                .then_inc(hid_read, 1)

            @block.vector
            def _(dve):
                for r in rounds(dve, NE // 2):
                    for e, k, c, par, n in chunks(r):
                        for a in range(2):
                            dve.wait_ge(turned, 2 * n + a + 1)
                            nc.vector.tensor_copy(xT[par][:, a, :], turn[a][:, :]).then_inc(xT_ready, 1)
                        if c == 0:
                            dve.wait_ge(w_in[k], 48 * r + 48)
                            nc.vector.tensor_copy(b1[k][:, :], C["b1"][:, bass.ds(e * NF, NF)]).then_inc(biases, 1)
                            for s in range(2):
                                last = nc.vector.tensor_scalar(b2s[k][:, s, :], b2[k][:, :], 0.8, None, ALU.mult)
                            last.then_inc(biases, 1)
                            dve.wait_ge(biases, 2 * e + 2)
                        need(dve, y_out[par], 8 * (n - par))
                        for t in range(2):
                            dve.wait_ge(res_full, 2 * n + t + 1)
                            nc.vector.scalar_tensor_tensor(
                                y[par][:, 2 * t:2 * t + 2, :].rearrange("p s n -> p (s n)"),
                                res[t][:, :, :].rearrange("p s n -> p (s n)"), 0.8,
                                b2s[k][:, :, :].rearrange("p s n -> p (s n)"), ALU.mult, ALU.add).then_inc(res_read, 1)



def combine(nc, C, D, io, scratch, out):
    NT = D["T"] // P
    R = 4
    with ExitStack() as ctx:
        sb, ps, sem = allocators(nc, ctx, "comb_")
        y = [[sb(f"y{i}_{k}", [P, 256]) for k in range(R)] for i in range(2)]
        xu = [sb(f"xu{k}", [P, 256]) for k in range(R)]
        half = [sb(f"half{k}", [P, 256]) for k in range(R)]
        done = [sb(f"done{k}", [P, 256]) for k in range(R)]
        index = [sb(f"index{k}", [P, 2], I32) for k in range(R)]
        y_in, xu_in, out_sent = ([sem(f"{n}{k}") for k in range(R)] for n in ("y_in", "xu_in", "out_sent"))
        index_ready, half_ready, ready = sem("index_ready"), sem("half_ready"), sem("ready")
        with nc.Block() as block:
            @block.sync
            def _(sp):
                for r in rounds(sp, NT // R):
                    for k in range(R):
                        need(sp, out_sent[k], 16 * r)
                        sp.dma_start(xu[k][:, :], scratch["xu"][bass.ds((R * r + k) * P, P), :]).then_inc(xu_in[k], 16)

            @block.gpsimd
            def _(pool):
                for r in rounds(pool, NT // R):
                    for k in range(R):
                        hold(pool, index_ready, R * r + k + 1, C["passed"])
                        for i in range(2):
                            nc.gpsimd.indirect_dma_start(
                                y[i][k][:, :], None, scratch["yslots"], bass.IndirectOffsetOnAxis(index[k][:, i:i + 1], 0),
                                bounds_check=NE * D["CAP"] - 1, oob_is_err=False).then_inc(y_in[k], 16)

            @block.vector
            def _(dve):
                def indices(n, k):
                    for i in range(2):
                        last = nc.vector.tensor_copy(index[k][:, i:i + 1], C["gather"][i][:, bass.ds(n, 1)])
                    last.then_inc(index_ready, 1)

                for k in range(R):
                    indices(k, k)
                for r in rounds(dve, NT // R):
                    for k in range(R):
                        n = R * r + k
                        dve.wait_ge(xu_in[k], 16 * r + 16)
                        dve.wait_ge(y_in[k], 32 * r + 32)
                        nc.vector.scalar_tensor_tensor(half[k][:, :], y[0][k][:, :], C["gate"][0][:, bass.ds(n, 1)],
                                                       xu[k][:, :], ALU.mult, ALU.add).then_inc(half_ready, 1)
                        dve.wait_ge(half_ready, n + 1)
                        need(dve, out_sent[k], 16 * r)
                        nc.vector.scalar_tensor_tensor(done[k][:, :], y[1][k][:, :], C["gate"][1][:, bass.ds(n, 1)],
                                                       half[k][:, :], ALU.mult, ALU.add).then_inc(ready, 1)
                        dve.wait_ge(ready, n + 1)
                        indices(n + R, k)

            @block.scalar
            def _(act):
                for r in rounds(act, NT // R):
                    for k in range(R):
                        act.wait_ge(ready, R * r + k + 1)
                        act.dma_start(out[bass.ds((R * r + k) * P, P), :], done[k][:, :]).then_inc(out_sent[k], 16)
                for k in range(R):
                    act.wait_ge(out_sent[k], 16 * (NT // R))



def program(nc, io, out):
    B = io["x"].shape[0] // 256
    T = B * 256
    CAP = -(-T // 4)
    D = {"B": B, "T": T, "CAP": CAP, "SLOTS": NE * CAP, "CLEARS": 16}
    ctx = ExitStack()
    with ctx:
        sb, ps, sem = allocators(nc, ctx, "")

        def dram(name, shape, dtype=F32):
            return nc.dram_tensor(name, shape, dtype).ap()

        scratch = {n: dram("d_" + n, [T, 256]) for n in ("y", "x1", "x2", "z", "xu", "h2")}
        scratch["q"], scratch["k"] = dram("d_q", [3, 256, 256], BF16), dram("d_k", [3, 256, 256], BF16)
        scratch["slots"], scratch["yslots"] = dram("d_slots", [NE * CAP, 256]), dram("d_yslots", [NE * CAP, 256])
        C = {
            "slots_cleared": sem("slots_cleared"), "passed": sem("passed"), "b1": sb("b1", [P, NE * 8]),
            "gather": [sb(f"gather{i}", [P, 2 * B + 4], I32) for i in range(2)],
            "scatter": [sb(f"scatter{i}", [P, 2 * B], I32) for i in range(2)],
            "gate": [sb(f"gate{i}", [P, 2 * B]) for i in range(2)],
            "ident_f": sb("ident_f", [P, P]), "ident_b": sb("ident_b", [P, P], BF16),
            "causal": sb("causal", [P, 2 * P], BF16), "below": sb("below", [P, P], BF16),
            "ones_b": sb("ones_b", [P, P], BF16), "wscale": sb("wscale", [P, 4]), "wT": sb("wT", [P, 4, 2, 256], BF16),
            "QS": [sb(f"QS{i}", [98, H, 256], BF16) for i in range(2)],
            "KS": [sb(f"KS{i}", [98, H, 256], BF16) for i in range(2)],
            "V": [sb(f"V{i}", [P, 2, H, VW]) for i in range(2)], "xmean": sb("xmean", [P, 2 * B]), "xrstd": sb("xrstd", [P, 2 * B]),
            "xscale": sb("xscale", [P, 1]), "qkv_scale": sb("qkv_scale", [P, 3]), "yscale": sb("yscale", [P, 1]),
            "xinv": sb("xinv", [P, 1]), "yinv": sb("yinv", [P, 1]),
            "yo_scale": sb("yo_scale", [P, 1]), "logits": sb("logits", [P, 2 * B, 8]),
        }
        C["columns"] = [("L0_attn_bq", "bq_a"), ("L0_attn_bk", "bk_a"), ("L0_ffn_bq", "bq_f"), ("L0_ffn_bk", "bk_f"),
                        ("L0_ffn_ln1_g", "ln1_g"), ("L0_ffn_ln1_b", "ln1_b")]
        C["broadcasts"] = [("L0_attn_bv", "bvA"), ("L0_ffn_bv", "bvF"), ("L0_attn_bo", "bo_a"), ("L0_xattn_bproj", "bproj"),
                           ("L0_ffn_bo", "bo_f"), ("L0_ffn_ln2_g", "ln2_g"), ("L0_ffn_ln2_b", "ln2_b")]
        C["matrices"] = [("L0_xattn_Wq", "xq", 256), ("L0_xattn_Wkv", "xkv", 512), ("L0_xattn_Wproj", "xo", 256),
                         ("L0_ffn_wq", "fq", 256), ("L0_ffn_wk", "fk", 256), ("L0_ffn_wv", "fv", 256),
                         ("L0_ffn_wo", "fo", 256), ("L0_ffn_wr", "wr", 8)]
        for name, key in C["columns"]:
            C[key] = sb(key, [P, 2])
        for name, key in C["broadcasts"]:
            C[key] = sb(key, [P, 2, 256]) if key[:2] != "bv" else sb(key, [P, 512])
        for name, key, n in C["matrices"]:
            C[key] = sb("w_" + key, [P, 2, n])
        C["columns"] = [(n, C[k][:, :]) for n, k in C["columns"]]
        C["broadcasts"] = [(n, C[k][:, j, :] if k[:2] != "bv" else C[k][:, j * 256:(j + 1) * 256])
                           for n, k in C["broadcasts"] for j in range(2)]
        C["matrices"] = [(n, C[k][:, :, :]) for n, k, _ in C["matrices"]]
        C["wA"] = [C["wT"][:, i, :, :] for i in range(3)] + [None]
        C["wX"] = [C["xq"], C["xkv"][:, :, 0:256], C["xkv"][:, :, 256:512], C["xo"]]
        C["wF"] = [C["fq"], C["fk"], C["fv"], C["fo"]]
        setup(nc, C, D, io, scratch["slots"])
        first_norm(nc, C, D, io)
        attention(nc, C, D, io, scratch, "A")
        attention(nc, C, D, io, scratch, "X")
        attention(nc, C, D, io, scratch, "F")
        route(nc, C, D, io)
        dispatch(nc, C, D, io, scratch)
        experts(nc, C, D, io, scratch)
        combine(nc, C, D, io, scratch, out)
def layout(inputs):
    import numpy as _np
    arrays = {}
    for name, a in inputs.items():
        a = _np.ascontiguousarray(a)
        if name == "x":
            a = a.reshape(-1, 256)
        if name == "ctx_1024":
            name, a = "ctx", a.reshape(-1, 256)
        if name == "mask_BxSxS2_bk0":
            name, a = "mask", a.reshape(-1, 120)
        if name in ("L0_ffn_w1", "L0_ffn_w2"):
            a = a.reshape(-1, a.shape[-1])
        arrays[name] = a
    return arrays



def kernel(**inputs):
    import concourse.bacc as bacc
    from concourse.bass_utils import run_bass_kernel_spmd

    shape = inputs["x"].shape
    nc = bacc.Bacc("TRN2", target_bir_lowering=False, num_devices=1)
    arrays, io = {}, {}
    for name, a in layout(inputs).items():
        arrays[f"in_{name}_dram"] = a
        io[name] = nc.dram_tensor(f"in_{name}_dram", a.shape, mybir.dt.from_np(a.dtype), kind="ExternalInput").ap()
    out = nc.dram_tensor("out_dram", [shape[0] * shape[1], shape[2]], F32, kind="ExternalOutput").ap()
    program(nc, io, out)
    result = run_bass_kernel_spmd(nc, [arrays], core_ids=[0])
    return result.results[0]["out_dram"].reshape(shape)
```

```python
import concourse.bass as bass
from concourse import mybir
from contextlib import ExitStack

F32, BF16, U8, I32 = mybir.dt.float32, mybir.dt.bfloat16, mybir.dt.uint8, mybir.dt.int32
ALU = mybir.AluOpType
ACT = mybir.ActivationFunctionType
AX = mybir.AxisListType
P = 128
MAGIC = 12582912.0
MASKED = -1e30
STACK = ((0, 3, 0), (3, 2, 1), (5, 1, 2))


def by_feature(w):
    return w.rearrange("p (h m d) -> p m d h", m=2, d=16)


def in_order(w):
    return w.rearrange("p (m d h) -> p m d h", m=2, d=16)


def need(eng, sem, value):
    if isinstance(value, int) and value <= 0:
        return
    eng.wait_ge(sem, value)


def hold(eng, sem, value, passed):
    need(eng, sem, value)
    if not isinstance(value, int):
        eng.sem_inc(passed, 1)


class Chain:

    def __init__(self, eng, sem, start, steps, passed):
        self.eng, self.sem, self.start, self.steps, self.passed, self.done = eng, sem, start, steps, passed, 0

    def step(self, instruction, apart=False):
        self.done += 1
        instruction.then_inc(self.sem, 1)
        if apart:
            hold(self.eng, self.sem, self.start + self.done, self.passed)
        else:
            self.eng.wait_ge(self.sem, self.start + self.done)

    def close(self):
        assert self.done == self.steps, (self.done, self.steps)


def rounds(eng, n):
    yield 0
    with eng.Fori(1, n) as r:
        yield r


def allocators(nc, ctx, prefix):
    def sb(name, shape, dtype=F32):
        return ctx.enter_context(nc.sbuf_tensor(prefix + name, shape, dtype))

    def ps(name, shape, dtype=F32):
        return ctx.enter_context(nc.psum_tensor(prefix + name, shape, dtype))

    sems = []

    def sem(name):
        sems.append(nc.alloc_semaphore(prefix + name))
        return sems[-1]

    def clear():
        nc.clear_and_free_semaphores(sems)
        nc.all_engine_barrier()

    if prefix:
        ctx.callback(clear)

    return sb, ps, sem


def rows(dram, b, n):
    return dram[bass.ds(b * n, n), :].rearrange("(j p) f -> p j f", p=P)


NEWTON = 3
CHAIN_OPS = 2 + 3 * NEWTON


def inverse_root(nc, i, var, y, t):
    v = nc.vector
    if i == 0:
        return v.tensor_scalar(t.bitcast(I32), var.bitcast(I32), 1, None, ALU.logical_shift_right)
    if i == 1:
        return v.tensor_scalar(y.bitcast(I32), t.bitcast(I32), -1.0, float(0x5F3759DF), ALU.mult, ALU.add)
    if i % 3 == 2:
        return v.tensor_tensor(t, y, y, ALU.mult)
    if i % 3 == 0:
        return v.scalar_tensor_tensor(t, t, -0.5, var, ALU.mult, ALU.mult)
    return v.scalar_tensor_tensor(y, t, 1.5, y, ALU.add, ALU.mult)



def setup(nc, C, D, io):
    with ExitStack() as ctx:
        sb, ps, sem = allocators(nc, ctx, "setup_")
        wraw = sb("wraw", [P, 4, 2, 256])
        wq = sb("wq", [P, 4, 2, 256])
        wint = sb("wint", [P, 4, 2, 256], BF16)
        wmax = sb("wmax", [P, 4])
        wmaxall, winv = sb("wmaxall", [P, 4]), sb("winv", [P, 4])
        wt_ps = ps("wt", [P, 2, 256], BF16)
        emptied = sem("emptied")
        loaded, pooled, wabs, wall, ints, turned, kept, link = (
            sem(n) for n in ("loaded", "pooled", "wabs", "wall", "ints", "turned", "kept", "link"))
        weights = [io["L0_attn_Wq"], io["L0_attn_Wk"], io["L0_attn_Wv"], io["L0_attn_Wo"]]
        loads = []
        for i, w in enumerate(weights):
            loads.append((wraw[:, i, :, :], w.rearrange("(j p) f -> p j f", p=P)))
        for name, dst in C["columns"]:
            loads.append((dst, io[name].rearrange("(m p) -> p m", p=P)))
        turned_in = [(C[key], sb("raw_" + key, [P, 2, 256])) for name, key in C["ordered"]]
        for (name, key), (dst, raw) in zip(C["ordered"], turned_in):
            w = io[name] if name != "L0_xattn_Wkv" else io[name][:, 0:256]
            loads.append((raw[:, :, :], w.rearrange("(c p) f -> p c f", p=P)))
        for name, dst in C["biases"]:
            loads.append((dst, io[name].rearrange("(h m d) -> d h m", m=2, d=16)))
        for name, dst in C["broadcasts"]:
            loads.append((dst, io[name].rearrange("(o f) -> o f", o=1).partition_broadcast(P)))
        for name, dst in C["matrices"]:
            w = io[name] if name != "L0_xattn_Wkv" else io[name][:, 256:512]
            loads.append((dst, w.rearrange("(c p) f -> p c f", p=P)))
        with nc.Block() as block:
            @block.sync
            def _(sp):
                for dst, src in loads:
                    sp.dma_start(dst, src, allow_slow_non_contiguous=True).then_inc(loaded, 16)
                sp.wait_ge(loaded, 16 * len(loads))

            @block.gpsimd
            def _(pool):
                nc.gpsimd.memset(C["ident_f"][:, :], 0.0).then_inc(pooled, 1)
                nc.gpsimd.memset(C["ident_b"][:, :], 0.0).then_inc(pooled, 1)
                nc.gpsimd.memset(C["causal"][:, :], 0.0).then_inc(pooled, 1)
                nc.gpsimd.memset(C["below"][:, :], 1.0).then_inc(pooled, 1)
                nc.gpsimd.memset(C["ones_b"][:, :], 1.0).then_inc(pooled, 1)
                pool.wait_ge(pooled, 5)
                for m in (C["ident_f"], C["ident_b"]):
                    nc.gpsimd.affine_select(out=m[:, :], in_=m[:, :], compare_op=ALU.not_equal, fill=1.0, base=0,
                                            pattern=[[-1, P]], channel_multiplier=1).then_inc(pooled, 1)
                for h in range(2):
                    half = C["causal"][:, h * P:(h + 1) * P]
                    nc.gpsimd.affine_select(out=half, in_=half, compare_op=ALU.is_ge, fill=MASKED, base=0,
                                            pattern=[[-1, P]], channel_multiplier=1).then_inc(pooled, 1)
                nc.gpsimd.affine_select(out=C["below"][:, :], in_=C["below"][:, :], compare_op=ALU.is_ge, fill=0.0,
                                        base=0, pattern=[[1, P]], channel_multiplier=-1).then_inc(pooled, 1)
                nc.gpsimd.iota(C["number"][:, :], [[P, D["T"] // P]], base=0, channel_multiplier=1).then_inc(pooled, 1)
                pool.wait_ge(pooled, 11)
                pool.wait_ge(wabs, 4)
                nc.gpsimd.partition_all_reduce(wmaxall[:, :], wmax[:, :], P, bass.bass_isa.ReduceOp.max)\
                    .then_inc(wall, 1)
                pool.wait_ge(wall, 1)

            @block.vector
            def _(dve):
                nc.vector.memset(C["empty"][:, :, :], 0.0).then_inc(emptied, 1)
                dve.wait_ge(emptied, 1)
                nc.vector.memset(C["empty"][:, :, 256:257].bitcast(I32), 2 ** 30).then_inc(emptied, 1)
                dve.wait_ge(emptied, 2)
                chain = Chain(dve, link, 0, 14, C["passed"])
                dve.wait_ge(loaded, 16 * len(loads))
                for i in range(4):
                    nc.vector.tensor_reduce(wmax[:, i:i + 1], wraw[:, i, :, :], AX.XY, ALU.max,
                                            apply_absolute_value=True).then_inc(wabs, 1)
                dve.wait_ge(wall, 1)
                chain.step(nc.vector.tensor_scalar(C["wscale"][:, :], wmaxall[:, :], 1.0 / 127.0, 1e-8, ALU.mult, ALU.max))
                chain.step(nc.vector.reciprocal(winv[:, :], C["wscale"][:, :]))
                for i in range(4):
                    chain.step(nc.vector.tensor_scalar(wq[:, i, :, :], wraw[:, i, :, :], winv[:, i:i + 1], MAGIC,
                                                       ALU.mult, ALU.add))
                    chain.step(nc.vector.tensor_scalar(wq[:, i, :, :], wq[:, i, :, :], MAGIC + 127.0, MAGIC - 128.0,
                                                       ALU.min, ALU.max))
                    nc.vector.tensor_scalar(wint[:, i, :, :], wq[:, i, :, :], MAGIC, None, ALU.subtract)\
                        .then_inc(ints, 1)
                for dst, raw in turned_in:
                    for c in range(2):
                        nc.vector.tensor_copy(in_order(dst[:, c, :]), by_feature(raw[:, c, :]))
                chain.step(nc.vector.tensor_scalar(C["bq_a"][:, :], C["bq_a"][:, :], 0.25, None, ALU.mult))
                chain.step(nc.vector.tensor_scalar(C["bq_f"][:, :], C["bq_f"][:, :], 0.25, None, ALU.mult))
                for kb in C["KS"]:
                    nc.vector.memset(kb[96:98, :, :], -1.0)
                chain.step(nc.vector.memset(C["V"][0][:, :, :, :], 0.0))
                chain.step(nc.vector.memset(C["V"][1][:, :, :, :], 0.0))
                nc.vector.memset(C["V"][0][:, :, :, 16:17], 1.0)
                nc.vector.memset(C["V"][1][:, :, :, 16:17], 1.0).then_inc(kept, 4)
                for i in range(4):
                    dve.wait_ge(turned, i + 1)
                    for c in range(2):
                        if i < 2:
                            last = nc.vector.tensor_copy(in_order(C["wT"][:, i, c, :]), by_feature(wt_ps[:, c, :]))
                        else:
                            last = nc.vector.tensor_copy(C["wT"][:, i, c, :], wt_ps[:, c, :])
                    last.then_inc(kept, 1)
                dve.wait_ge(kept, 8)

            @block.tensor
            def _(pe):
                pe.wait_ge(pooled, 10)
                for i in range(4):
                    pe.wait_ge(ints, i + 1)
                    if i:
                        pe.wait_ge(kept, 4 + i)
                    for c in range(2):
                        for j in range(2):
                            last = nc.tensor.transpose(wt_ps[:, c, j * P:(j + 1) * P],
                                                       wint[:, i, j, c * P:(c + 1) * P], C["ident_b"][:, :])
                    last.then_inc(turned, 1)



def first_norm(nc, C, D, io):
    B, NT = D["B"], D["T"] // P
    with ExitStack() as ctx:
        sb, ps, sem = allocators(nc, ctx, "norm_")
        x = [sb(f"x{i}", [P, 2, 256]) for i in range(2)]
        stats, pair = [[sb(f"{n}{i}", [P, 2, w]) for i in range(2)] for n, w in (("stats", 6), ("pair", 2))]
        mean_var, ends = sb("mean_var", [P, NT, 2]), sb("ends", [P, 2, NT])
        root, far = sb("root", [P, 2, NT]), sb("far", [P, 2, NT])
        best, best_all = sb("best", [P, 1]), sb("best_all", [P, 1])
        x_in = [sem(f"x_in{i}") for i in range(2)]
        partial, x_read, link, reduced = (sem(n) for n in ("partial", "x_read", "link", "reduced"))
        with nc.Block() as block:
            @block.sync
            def _(sp):
                for r in rounds(sp, B // 2):
                    for k in range(2):
                        need(sp, x_read, 2 * r + k - 1)
                        sp.dma_start(x[k][:, :, :], rows(io["x"], 2 * r + k, 256)).then_inc(x_in[k], 16)

            @block.vector
            def _(dve):
                v = nc.vector
                for r in rounds(dve, B // 2):
                    for k in range(2):
                        b = 2 * r + k
                        dve.wait_ge(x_in[k], 16 * r + 16)
                        v.bn_stats(stats[k][:, 0, :], x[k][:, 0, :])
                        v.bn_stats(stats[k][:, 1, :], x[k][:, 1, :]).then_inc(partial, 1)
                        v.tensor_reduce(ends[:, 0, bass.ds(2 * b, 2)], x[k][:, :, :], AX.X, ALU.max)
                        v.tensor_reduce(ends[:, 1, bass.ds(2 * b, 2)], x[k][:, :, :], AX.X, ALU.min).then_inc(x_read, 1)
                        hold(dve, partial, 2 * b + 1, C["passed"])
                        v.bn_aggr(pair[k][:, 0, :], stats[k][:, 0, :])
                        v.bn_aggr(pair[k][:, 1, :], stats[k][:, 1, :]).then_inc(partial, 1)
                        dve.wait_ge(partial, 2 * b + 2)
                        v.tensor_copy(mean_var[:, bass.ds(2 * b, 2), :], pair[k][:, :, :]).then_inc(link, 1)
                dve.wait_ge(x_read, B)
                dve.wait_ge(link, B)
                chain = Chain(dve, link, B, 4 + CHAIN_OPS, C["passed"])
                chain.step(v.tensor_copy(C["xmean"][:, :], mean_var[:, :, 0]))
                chain.step(v.tensor_scalar(root[:, 0, :], mean_var[:, :, 1], 1e-5, None, ALU.add))
                for i in range(CHAIN_OPS):
                    chain.step(inverse_root(nc, i, root[:, 0, :], C["xrstd"][:, :], root[:, 1, :]))
                wide = C["xmean"][:, :].unsqueeze(1).broadcast_to([P, 2, NT])
                chain.step(v.tensor_tensor(far[:, :, :], ends[:, :, :], wide, ALU.subtract))
                wide = C["xrstd"][:, :].unsqueeze(1).broadcast_to([P, 2, NT])
                chain.step(v.tensor_tensor(far[:, :, :], far[:, :, :], wide, ALU.mult))
                v.tensor_reduce(best[:, :], far[:, :, :], AX.XY, ALU.max, apply_absolute_value=True).then_inc(reduced, 1)
                chain.close()
                dve.wait_ge(reduced, 2)
                v.tensor_scalar(C["xscale"][:, :], best_all[:, :], 1.0 / 127.0, 1e-8, ALU.mult, ALU.max).then_inc(reduced, 1)
                dve.wait_ge(reduced, 3)
                v.reciprocal(C["xinv"][:, :], C["xscale"][:, :]).then_inc(reduced, 1)
                for i, extra in enumerate((0.25, 1.0, 1.0)):
                    v.tensor_scalar(C["qkv_scale"][:, i:i + 1], C["xscale"][:, :], C["wscale"][:, i:i + 1], extra,
                                    ALU.mult, ALU.mult).then_inc(reduced, 1)
                dve.wait_ge(reduced, 7)

            @block.gpsimd
            def _(pool):
                pool.wait_ge(reduced, 1)
                nc.gpsimd.partition_all_reduce(best_all[:, :], best[:, :], P, bass.bass_isa.ReduceOp.max)\
                    .then_inc(reduced, 1)
                pool.wait_ge(reduced, 2)

H, HD, VW = 16, 16, 32


SCHEDULE = {
    "A": ["pv3 evac3 v", "", "tok0 xT0", "", "xT1 tok1", "q pv0 maxima evac0", "q_rest maxima maxima maxima maxima",
          "maxima maxima k maxima maxima maxima", "maxima q_store maxima k_rest maxima maxima maxima",
          "maxima pv1 evac1", "top k_store", "rows", "", "pv2 evac2", "", "norm"],
    "X": ["pv3 v evac3 tok0 tok1", "", "norm ctxT xT q pv0 maxima maxima yT", "maxima wo q_rest k q_store stats",
          "maxima aggr", "var maxima c0 c1 evac0 k_rest maxima maxima pv1 evac1 c2 c3", "maxima c4 c5 top aT pv2",
          "c6 k_store c7 c8 rows proj c9 c10 apply evac2"],
    "F": ["pv3 v evac3", "tok0", "xT tok1", "", "maxima maxima maxima q maxima", "aT maxima maxima",
          "maxima h2T0 pv0 maxima maxima q_rest", "maxima stats evac0 proj", "maxima k aggr ustats",
          "maxima h2T1 maxima pv1 var maxima maxima", "uaggr route uvar c0 k_rest q_store", "maxima c1 evac1", "c2",
          "top k_store c3 pv2 c4 evac2", "c5 c6 c7 rows c8", "c9 c10 uapply apply"],
}


BANKS = {"A": (3, 2), "X": (3, 2), "F": (3, 2)}


def attention(nc, C, D, io, scratch, kind):
    B = D["B"]
    KN = 121 if kind == "X" else 256
    KT = 120 if kind == "X" else 256
    KR = KN if kind == "X" else P
    TCOL = {"A": 384, "X": 256, "F": 512}[kind]
    q_dram, k_dram = scratch["q"], scratch["k" if KT == 256 else "k120"]
    QS, KS, V = C["QS"], C["KS"], C["V"]
    ident_f, ident_b = C["ident_f"], C["ident_b"]
    NEWTON_OPS = ["c%d" % i for i in range(CHAIN_OPS)]

    HB = 2 if kind == "X" else 1
    G = H // HB

    STEPS = [("load", 0), ("refetch", 0), ("fetch", 0)]
    groups = 0
    for i, names in enumerate(SCHEDULE[kind]):
        STEPS.append(("attend", i))
        for name in names.split():
            STEPS.append((name, groups if name == "maxima" else 0))
            groups += name == "maxima"
    assert groups == G and len(SCHEDULE[kind]) == G

    SB, TB = BANKS[kind]

    def earlier(g, i, banks):
        return G * g + i - banks + 1 if i >= banks else G * (g - 1) + (G - 1 - i) // banks * banks + i + 1

    LAG = {"load": 1, "v": 1, "maxima": 1, "top": 1, "rows": 1, "attend": 0, "pv0": 0, "pv1": 0, "pv2": 0, "evac0": 0, "evac1": 0, "evac2": 0,
           "pv3": -1, "evac3": -1, "refetch": -1, "tok0": -1, "tok1": -1, "aT": -1, "proj": -1,
           "ustats": -1, "uaggr": -1, "uvar": -1, "uapply": -1, "h2T0": -2, "h2T1": -2, "route": -2,
           "ctxT": 2, "xT0": 2, "xT1": 2, "xT": 2, "q": 2, "q_rest": 2, "q_store": 2, "k": 2, "k_rest": 2, "k_store": 2,
           "fetch": 3, "norm": 3, "yT": 3, "wo": 3, "stats": 3, "aggr": 3, "var": 3, "apply": 3}
    LAG.update({c: 3 for c in NEWTON_OPS})
    TURNS = {c: B + 4 if kind == "F" else B for c in NEWTON_OPS}
    UNITS = [n for n, _ in STEPS if n in ("v", "ctxT", "xT0", "xT1", "xT", "q", "k", "yT", "wo", "tok0", "tok1", "aT", "proj",
                                          "h2T0", "h2T1", "route", "rows")]
    NU = len(UNITS)
    assert NU % 2 == 0
    LINKS = {"top": 3, "norm": {"A": 3, "X": 2, "F": 0}[kind], "stats": 1, "aggr": 1, "var": 1, "ustats": 1, "uaggr": 1,
             "uvar": 1, "tok0": 1, "tok1": 3 if kind == "A" else 1}
    LINKS.update({c: 1 for c in NEWTON_OPS})

    def turns(b, name):
        return b + LAG[name] if not isinstance(b, int) else min(max(b + LAG[name], 0), TURNS.get(name, B))

    def present(b, name):
        return not isinstance(b, int) or 0 <= b + LAG[name] < TURNS.get(name, B)

    def total(b, counts):
        if isinstance(b, int):
            return sum(turns(b, n) * c for n, c in counts)
        return b * sum(c for _, c in counts) + sum(LAG[n] * c for n, c in counts)

    def filling(b, name):
        if isinstance(b, int):
            n = total(b, [(u, 1) for u in UNITS]) + sum(present(b, u) for u in UNITS[:UNITS.index(name)])
            return n % 2, n // 2
        base = sum(LAG[u] for u in UNITS) + UNITS.index(name)
        return base % 2, NU // 2 * b + base // 2

    ORDER = [n for n, _ in STEPS if n in LINKS]

    def linked(b, name):
        return total(b, [(n, LINKS[n]) for n in ORDER]) + \
            sum(LINKS[n] for n in ORDER[:ORDER.index(name)] if present(b, n))

    FIRST, LAST = -3, B - min(LAG[n] for n, _ in STEPS) - 1

    def iterations(eng):
        for b in range(FIRST, 3):
            yield b, b % 2
        with eng.Fori(0, (B - 6) // 2) as r:
            yield 2 * r + 3, 1
            yield 2 * r + 4, 0
        for b in range(B - 3, LAST + 1):
            yield b, b % 2

    def steps(b, par):
        for name, i in STEPS:
            if present(b, name):
                yield name, i, b + LAG[name], (par + LAG[name]) % 2

    with ExitStack() as ctx:
        sb, ps, sem = allocators(nc, ctx, kind + "_")
        work = [ps(f"work{i}", [P, 512]) for i in range(2)]
        score = [ps(f"score{i}", [P, 512]) for i in range(SB)]
        scoreT = [ps(f"scoreT{i}", [P, 512]) for i in range(TB)]
        outs = ps("outs", [P, 256])
        probs = [sb(f"probs{i}", [P, 4, TCOL]) for i in range(2)]
        outT = sb("outT", [P, 4, 256])
        tok, rec = sb("tok", [P, 2, 256]), sb("rec", [P, 2, H])
        tops, top2 = sb("tops", [P, 3, H]), sb("top2", [P, 2, H])
        top_parts, top_rows = sb("top_parts", [P, 2, 2, H], BF16), sb("top_rows", [32, 256], BF16)
        xdt = BF16 if kind == "A" else F32
        xin, grid = sb("xin", [P, 2, 256]), sb("grid", [P, 2, 256])
        xw, xT = sb("xw", [P, 2, 256], xdt), sb("xT", [P, 2, 256], xdt)
        q_f, k_f, left = sb("q_f", [P, 2, 256]), sb("k_f", [P, 2, 256]), sb("left", [P, 2, 256])
        q_parts, k_parts = sb("q_parts", [P, 3, 2, 256], BF16), sb("k_parts", [P, 3, 2, KT], BF16)
        NR = 6 if kind == "F" else 2
        stats, mean_var, rstd = sb("stats", [P, 2, 6]), sb("mean_var", [P, 2, 2]), sb("rstd", [P, 3, NR])
        aT, xres, zres = sb("aT", [P, 2, 256]), sb("xres", [P, 2, 256]), sb("zres", [P, 2, 256])
        based, summed = sb("based", [P, 2, 256]), sb("summed", [P, 2, 256])
        work_full, work_drained = [[sem(f"{n}{i}") for i in range(2)] for n in ("work_full", "work_drained")]
        (x_in, normed, q_cast0, q_rest, q_cast1, q_split, q_out, k_cast0, k_rest, k_cast1, k_split, k_out, stack_in,
         score_full, score_read, rows_in, scoreT_full, probs_full, pv_done, outs_read, link_v, result_out) = (
             sem(n) for n in ("x_in", "normed", "q_cast0", "q_rest", "q_cast1", "q_split", "q_out", "k_cast0", "k_rest",
                              "k_cast1", "k_split", "k_out", "stack_in", "score_full", "score_read", "rows_in",
                              "scoreT_full", "probs_full", "pv_done", "outs_read", "link_v", "result_out"))
        if kind == "A":
            absmax, best, best_all = sb("absmax", [P, 1]), sb("best", [P, 1]), sb("best_all", [P, 1])
            reduced = sem("reduced")
        if kind == "X":
            yin, yint, yT = sb("yin", [P, 2, 256]), sb("yint", [P, 2, 256], BF16), sb("yT", [P, 2, 256], BF16)
            xb, x1, cin, ctxT = sb("xb", [P, 2, 256]), sb("x1", [P, 2, 256]), sb("cin", [120, 256]), sb("ctxT", [P, 2, 120])
            mraw, mask = sb("mraw", [P, 2, 120], U8), [sb(f"mask{i}", [P, 2, KN], BF16) for i in range(2)]
            zeroed = sem("zeroed")
            y_in, y_ready, ctx_in, mask_in, mask_ready, xb_ready, x1_out, xres_in, based_ready, mask_zero = (
                sem(n) for n in ("y_in", "y_ready", "ctx_in", "mask_in", "mask_ready", "xb_ready", "x1_out", "xres_in",
                                 "based_ready", "mask_zero"))
        if kind == "F":
            z, hn, h2, h2T = sb("z", [P, 2, 256]), sb("hn", [P, 2, 256]), sb("h2", [P, 2, 256]), sb("h2T", [P, 2, 256])
            xu = sb("xu", [P, 2, 256])
            ustats, umean_var, rstd_set = sb("ustats", [P, 2, 6]), sb("umean_var", [P, 2, 2]), sem("rstd_set")
            z_out, zres_in, xres_in, based_ready, hn_ready, xu_ready, h2_ready, h2_out = (
                sem(n) for n in ("z_out", "zres_in", "xres_in", "based_ready", "hn_ready", "xu_ready", "h2_ready", "h2_out"))

        with nc.Block() as block:
            @block.sync
            def _(sp):
                def drained(b, name):
                    if present(b, name):
                        bank, use = filling(b, name)
                        need(sp, work_drained[bank], use + 1)

                if kind == "X":
                    sp.dma_start(cin[:, :], io["ctx"][0:120, :]).then_inc(ctx_in, 16)
                for b, par in iterations(sp):
                    for name, i, g, gp in steps(b, par):
                        if name == "load":
                            hold(sp, q_out, 16 * g + 16, C["passed"])
                            hold(sp, k_out, 16 * g + 16, C["passed"])
                            need(sp, scoreT_full, G * (g - 1))
                            for first, blocks, part in STACK:
                                sp.dma_start(QS[gp][16 * first:16 * (first + blocks), :, :],
                                             q_dram[part, :, :].unsqueeze(0).broadcast_to([blocks, HD, H * 256]))\
                                    .then_inc(stack_in, 16)
                                sp.dma_start(KS[gp][16 * first:16 * (first + blocks), :, 0:KT],
                                             k_dram[0:blocks, :, :].rearrange("a d x -> (a d) x")).then_inc(stack_in, 16)
                            if kind == "X":
                                hold(sp, mask_ready, g, C["passed"])
                                sp.dma_start(mraw[:, :, :], rows(io["mask"], g, 256)).then_inc(mask_in, 16)
                        if name == "fetch":
                            need(sp, xb_ready if kind == "X" else normed, g)
                            src = scratch["x2"] if kind == "F" else io["x"]
                            sp.dma_start(xin[:, :, :], rows(src, g, 256)).then_inc(x_in, 16)
                            if kind == "X":
                                need(sp, y_ready, g)
                                sp.dma_start(yin[:, :, :], rows(scratch["y"], g, 256)).then_inc(y_in, 16)
                        if name == "xT" and kind == "X":
                            drained(b, "ctxT")
                            if not isinstance(b, int) or present(b + 1, "xT"):
                                sp.dma_start(cin[:, :], io["ctx"][bass.ds((g + 1) * 120, 120), :]).then_inc(ctx_in, 16)
                        if name == "refetch" and kind == "X":
                            need(sp, x1_out, 16 * g + 16)
                            need(sp, based_ready, g)
                            sp.dma_start(xres[:, :, :], rows(scratch["x1"], g, 256)).then_inc(xres_in, 16)
                        if name == "refetch" and kind == "F":
                            need(sp, z_out, 16 * g + 16)
                            need(sp, based_ready, g)
                            sp.dma_start(zres[:, :, :], rows(scratch["z"], g, 256)).then_inc(zres_in, 16)
                            need(sp, xu_ready, g)
                            sp.dma_start(xres[:, :, :], rows(scratch["x2"], g, 256)).then_inc(xres_in, 16)
                        if name == "fetch" and kind == "A":
                            sp.dma_start(scratch["slots"][bass.ds(g * D["CLEARED"], D["CLEARED"]), :].rearrange(
                                "(j p) f -> p j f", p=P), C["empty"][:, :, :]).then_inc(C["slots_cleared"], 16)
                        if name == "tok1" and kind == "A":
                            drained(b, "tok1")
                            sp.dma_start(rows(scratch["y"], g, 256), tok[:, :, :]).then_inc(result_out, 16)
                        if name == "proj" and kind == "X":
                            drained(b, "proj")
                            sp.dma_start(rows(scratch["x2"], g, 256), summed[:, :, :]).then_inc(result_out, 16)
                        if name == "uapply":
                            sp.wait_ge(xu_ready, g + 1)
                            sp.dma_start(rows(scratch["out"], g, 256), xu[:, :, :]).then_inc(result_out, 16)
                            sp.wait_ge(h2_ready, 2 * g + 2)
                            sp.dma_start(rows(scratch["h2"], g, 256), h2[:, :, :]).then_inc(h2_out, 16)
                        if name == "stats" and kind == "X":
                            drained(b, "wo")
                            sp.dma_start(rows(scratch["x1"], g, 256), x1[:, :, :]).then_inc(x1_out, 16)
                        if name == "apply" and kind == "F":
                            sp.wait_ge(normed, g + 1)
                            sp.dma_start(rows(scratch["z"], g, 256), z[:, :, :]).then_inc(z_out, 16)
                        if name in ("q_store", "k_store"):
                            split, out, parts, n = (q_split, q_out, q_parts, 256) if name[0] == "q" else \
                                (k_split, k_out, k_parts, KT)
                            hold(sp, split, g + 1, C["passed"])
                            need(sp, stack_in, 96 * g)
                            dst = q_dram if name[0] == "q" else k_dram
                            sp.dma_start(dst.rearrange("a d (h x) -> (d h) a x", h=H // 2), parts[:, :, :, :].rearrange(
                                "p a m t -> p a (m t)")).then_inc(out, 16)
                        if name == "rows":
                            drained(b, "rows")
                            for part in range(2):
                                sp.dma_start(QS[gp][96 + part:97 + part, :, :], top_rows[16 * part:16 * part + 16, :])\
                                    .then_inc(rows_in, 16)
                sp.wait_ge(result_out, 16 * B)
                sp.wait_ge(rows_in, 32 * B)
                if kind == "F":
                    sp.wait_ge(h2_out, 16 * B)
                if kind == "X":
                    sp.wait_ge(x1_out, 16 * B)

            @block.tensor
            def _(pe):
                mm = nc.tensor.matmul
                wq, wk, wv, wo = C["w" + kind]
                for b, par in iterations(pe):
                    for name, i, g, gp in steps(b, par):
                        if name in UNITS:
                            bank, use = filling(b, name)
                            W = work[bank]

                        def drained(*names):
                            last = {}
                            for n in names:
                                bk, us = filling(b, n)
                                last[bk] = us
                            for bk, us in last.items():
                                if bk != bank:
                                    need(pe, work_drained[bk], us + 1)

                        if name == "attend":
                            s = scoreT[i % TB]
                            if i == 0:
                                pe.wait_ge(rows_in, 32 * g + 32)
                            need(pe, probs_full, earlier(g, i, TB))
                            q, k = QS[gp], KS[gp]
                            if kind == "A":
                                for n in range(2):
                                    mm(s[:, n * P:(n + 1) * P], C["causal"][:, 0:P], ident_b[:, :], start=n == 0,
                                       stop=False, skip_group_check=True)
                                mm(s[:, 0:P], k[0:98, i, P:256], q[0:98, i, P:256], start=False, stop=False,
                                   skip_group_check=True)
                                last = mm(s[:, P:384], k[0:98, i, 0:P], q[0:98, i, :], start=False, stop=True,
                                          skip_group_check=True)
                            elif kind == "X":
                                for u in range(HB):
                                    for n in range(2):
                                        mm(s[0:KN, u * 256 + n * P:u * 256 + (n + 1) * P], mask[gp][:, n, :], ident_b[:, :],
                                           start=u + n == 0, stop=False, skip_group_check=True)
                                for u in range(HB):
                                    last = mm(s[0:KN, u * 256:(u + 1) * 256], k[0:98, HB * i + u, 0:KN], q[0:98, HB * i + u, :],
                                              start=False, stop=u == HB - 1, skip_group_check=True)
                            else:
                                for n in range(2):
                                    last = mm(s[:, n * 256:(n + 1) * 256], k[0:98, i, n * P:(n + 1) * P], q[0:98, i, :],
                                              start=True, stop=True)
                            last.then_inc(scoreT_full, 1)
                        if name == "maxima":
                            s = score[i % SB]
                            if i == 0:
                                pe.wait_ge(stack_in, 96 * g + 96)
                                if kind == "X":
                                    pe.wait_ge(zeroed, 1)
                                    pe.wait_ge(mask_ready, g + 1)
                            need(pe, score_read, earlier(g, i, SB))
                            q, k = QS[gp], KS[gp]
                            if kind == "A":
                                mm(s[:, P:384], ident_b[:, :], C["causal"][:, :], start=True, stop=False,
                                   skip_group_check=True)
                                mm(s[:, 0:256], q[0:96, i, P:256], k[0:96, i, :], start=False, stop=False,
                                   skip_group_check=True)
                                last = mm(s[:, 256:384], q[0:96, i, 0:P], k[0:96, i, 0:P], start=False, stop=True,
                                          skip_group_check=True)
                            elif kind == "X":
                                for u in range(HB):
                                    mm(s[:, 2 * u * KN:2 * (u + 1) * KN], ident_b[:, :], mask[gp][:, :, :], start=u == 0,
                                       stop=False, skip_group_check=True)
                                for u in range(HB):
                                    for n in range(2):
                                        last = mm(s[:, (2 * u + n) * KN:(2 * u + n + 1) * KN],
                                                  q[0:96, HB * i + u, n * P:(n + 1) * P], k[0:96, HB * i + u, 0:KN],
                                                  start=False, stop=u + n == HB, skip_group_check=True)
                            else:
                                for n in range(2):
                                    last = mm(s[:, n * 256:(n + 1) * 256], q[0:96, i, n * P:(n + 1) * P], k[0:96, i, :],
                                              start=True, stop=True)
                            last.then_inc(score_full, 1)
                        if name[:2] == "pv":
                            m = int(name[2])
                            if m == 0:
                                vb, vu = filling(b - 1, "v")
                                pe.wait_ge(work_drained[vb], vu + 1)
                            pe.wait_ge(probs_full, G * g + (m + 1) * 4 // HB)
                            need(pe, outs_read, 4 * g + m)
                            pr = probs[m % 2]
                            if kind == "A":
                                for n in range(2):
                                    for j in range(4):
                                        o = outs[32 * j:32 * j + 32, :] if n == 0 else outs[32 * j:32 * j + 32, P:256]
                                        x = pr[:, j, P:384] if n == 0 else pr[:, j, 0:P]
                                        last = mm(o, V[gp][:, n, 4 * m + j, :], x, start=n == 0, stop=n == 1,
                                                  skip_group_check=True)
                            elif kind == "X":
                                for j in range(4):
                                    last = mm(outs[32 * j:32 * j + 32, :], V[gp][0:KN, 0, 4 * m + j, :], pr[0:KN, j, :],
                                              start=True, stop=True)
                            else:
                                for n in range(2):
                                    for j in range(4):
                                        last = mm(outs[32 * j:32 * j + 32, :], V[gp][:, n, 4 * m + j, :],
                                                  pr[:, j, n * 256:(n + 1) * 256], start=n == 0, stop=n == 1,
                                                  skip_group_check=True)
                            last.then_inc(pv_done, 1)
                        if name not in UNITS:
                            continue
                        need(pe, work_drained[bank], use)
                        Wb = W[:, :].bitcast(BF16)
                        if name in ("xT0", "xT1"):
                            j = int(name[2])
                            pe.wait_ge(normed, g + 1)
                            for c in range(2):
                                last = nc.tensor.transpose(Wb[:, c * P:(c + 1) * P], xw[:, j, c * P:(c + 1) * P], ident_b[:, :])
                        elif name == "yT":
                            pe.wait_ge(y_ready, g + 1)
                            for c in range(2):
                                for j in range(2):
                                    last = nc.tensor.transpose(Wb[:, c * 256 + j * P:c * 256 + j * P + P],
                                                               yint[:, j, c * P:(c + 1) * P], ident_b[:, :])
                        elif name == "wo":
                            drained("yT")
                            for j in range(2):
                                for c in range(2):
                                    last = mm(W[:, j * 256:(j + 1) * 256], yT[:, c, j * P:(j + 1) * P], C["wT"][:, 3, c, :],
                                              start=c == 0, stop=c == 1)
                        elif name == "ctxT":
                            pe.wait_ge(ctx_in, 16 * g + 16)
                            for c in range(2):
                                last = nc.tensor.transpose(W[:, c * 120:(c + 1) * 120], cin[:, c * P:(c + 1) * P],
                                                           ident_f[0:120, 0:120])
                        elif name == "xT":
                            pe.wait_ge(normed, g + 1)
                            for c in range(2):
                                for j in range(2):
                                    last = nc.tensor.transpose(W[:, c * 256 + j * P:c * 256 + j * P + P],
                                                               xw[:, j, c * P:(c + 1) * P], ident_f[:, :])
                        elif name in ("q", "k"):
                            src, w, n = (xT, wq, 256) if name == "q" or kind != "X" else (ctxT, wk, KT)
                            w = wq if name == "q" else wk
                            drained("xT1" if kind == "A" else "ctxT" if src is not xT else "xT")
                            for m in range(2):
                                for c in range(2):
                                    last = mm(W[:, m * 256:m * 256 + n], w[:, c, m * P:(m + 1) * P], src[:, c, 0:n],
                                              start=c == 0, stop=c == 1)
                        elif name == "v":
                            if kind == "X":
                                for c in range(2):
                                    last = mm(W[0:120, 0:256], ctxT[:, c, :], wv[:, c, :], start=c == 0, stop=c == 1)
                            else:
                                for j in range(2):
                                    for c in range(2):
                                        last = mm(W[:, j * 256:(j + 1) * 256], xT[:, c, j * P:(j + 1) * P], wv[:, c, :],
                                                  start=c == 0, stop=c == 1)
                        elif name == "rows":
                            pe.wait_ge(link_v, linked(b, "top") + 3)
                            for j in range(2):
                                last = nc.tensor.transpose(Wb[0:32, j * P:(j + 1) * P],
                                                           top_parts[:, j, :, :].rearrange("p a h -> p (a h)"), ident_b[:, :])
                        elif name in ("tok0", "tok1"):
                            j = int(name[3])
                            pe.wait_ge(outs_read, 4 * g + 4)
                            for m in range(4):
                                last = nc.tensor.transpose(W[:, m * P:(m + 1) * P], outT[:, m, j * P:(j + 1) * P], ident_f[:, :])
                        elif name == "aT":
                            drained("tok0", "tok1")
                            for c in range(2):
                                for j in range(2):
                                    last = nc.tensor.transpose(W[:, c * 256 + j * P:c * 256 + j * P + P],
                                                               tok[:, j, c * P:(c + 1) * P], ident_f[:, :])
                        elif name == "proj":
                            drained("aT")
                            for j in range(2):
                                for c in range(2):
                                    last = mm(W[:, j * 256:(j + 1) * 256], aT[:, c, j * P:(j + 1) * P], wo[:, c, :],
                                              start=c == 0, stop=c == 1)
                        elif name in ("h2T0", "h2T1"):
                            c = int(name[3])
                            pe.wait_ge(h2_ready, 2 * g + 2)
                            for j in range(2):
                                last = nc.tensor.transpose(W[:, j * P:(j + 1) * P], h2[:, j, c * P:(c + 1) * P], ident_f[:, :])
                        elif name == "route":
                            drained("h2T0", "h2T1")
                            for j in range(2):
                                for c in range(2):
                                    last = mm(W[:, j * 8:(j + 1) * 8], h2T[:, c, j * P:(j + 1) * P], C["wr"][:, c, :],
                                              start=c == 0, stop=c == 1)
                        last.then_inc(work_full[bank], 1)

            @block.scalar
            def _(act):
                for b, par in iterations(act):
                    for name, i, g, gp in steps(b, par):
                        if name == "attend":
                            m, at = HB * i // 4, HB * i % 4
                            act.wait_ge(scoreT_full, G * g + i + 1)
                            if at == 0:
                                need(act, pv_done, 4 * g + m - 1)
                            nc.scalar.activation(probs[m % 2][0:KR, at:at + HB, :].rearrange("p u x -> p (u x)"),
                                                 scoreT[i % TB][0:KR, 0:HB * TCOL], ACT.Exp)\
                                .then_inc(probs_full, 1)
                        if name[:4] == "evac":
                            m = int(name[4])
                            act.wait_ge(pv_done, 4 * g + m + 1)
                            if m == 0 and present(b, "tok1"):
                                bk, us = filling(b, "tok1")
                                act.wait_ge(work_full[bk], us + 1)
                            nc.scalar.activation(outT[:, m, :], outs[:, :], ACT.Copy).then_inc(outs_read, 1)
                        if name not in ("xT0", "xT1", "xT", "yT", "ctxT", "q", "k", "rows", "aT", "h2T0", "h2T1", "q_rest", "k_rest"):
                            continue
                        if name in ("q_rest", "k_rest"):
                            rest, cast, parts, n = (q_rest, q_cast1, q_parts, 256) if name[0] == "q" else \
                                (k_rest, k_cast1, k_parts, KT)
                            act.wait_ge(rest, g + 1)
                            nc.scalar.activation(parts[:, 1, :, 0:n], left[:, :, 0:n], ACT.Copy).then_inc(cast, 1)
                            continue
                        bank, use = filling(b, name)
                        W, Wb = work[bank], work[bank][:, :].bitcast(BF16)

                        def drained(b, name):
                            if present(b, name):
                                bk, us = filling(b, name)
                                need(act, work_drained[bk], us + 1)

                        act.wait_ge(work_full[bank], use + 1)
                        if name in ("xT0", "xT1"):
                            j = int(name[2])
                            drained(b, "v")
                            last = nc.scalar.activation(xT[:, :, j * P:(j + 1) * P],
                                                        Wb[:, 0:256].rearrange("p (c t) -> p c t", c=2), ACT.Copy)
                        elif name == "yT":
                            drained(b - 1, "wo")
                            last = nc.scalar.activation(yT[:, :, :], Wb[:, 0:512].rearrange("p (c t) -> p c t", c=2), ACT.Copy)
                        elif name == "ctxT":
                            drained(b, "v")
                            last = nc.scalar.activation(ctxT[:, :, :], W[:, 0:240].rearrange("p (c t) -> p c t", c=2), ACT.Copy)
                        elif name == "xT" and kind == "X":
                            drained(b, "v")
                            last = nc.scalar.activation(xT[:, :, :], W[:, :].rearrange("p (c t) -> p c t", c=2), ACT.Copy)
                        elif name == "xT":
                            drained(b, "v")
                            for c in range(2):
                                last = nc.scalar.activation(xT[:, c, :], W[:, c * 256:(c + 1) * 256], ACT.Identity,
                                                            bias=C["ln1_b"][:, c:c + 1], scale=C["ln1_g"][:, c:c + 1])
                        elif name in ("q", "k"):
                            dst, split, parts, cast, out = (q_f, q_split, q_parts, q_cast0, q_out) if name == "q" else \
                                (k_f, k_split, k_parts, k_cast0, k_out)
                            n = 256 if name == "q" else KT
                            need(act, split, g)
                            for m in range(2):
                                src = W[:, m * 256:m * 256 + n]
                                if kind == "A":
                                    bias = C["bq_a" if name == "q" else "bk_a"][:, m:m + 1]
                                    scale = C["qkv_scale"][:, 0:1] if name == "q" else C["qkv_scale"][:, 1:2]
                                elif kind == "F":
                                    bias = C["bq_f" if name == "q" else "bk_f"][:, m:m + 1]
                                    scale = 0.25 if name == "q" else 1.0
                                if kind == "X":
                                    last = nc.scalar.activation(dst[:, m, 0:n], src, ACT.Copy, scale=0.25 if name == "q" else 1.0)
                                else:
                                    last = nc.scalar.activation(dst[:, m, 0:n], src, ACT.Identity, bias=bias, scale=scale)
                        elif name == "rows":
                            need(act, rows_in, 32 * g)
                            last = nc.scalar.activation(top_rows[:, :], Wb[0:32, 0:256], ACT.Copy)
                        elif name == "aT":
                            drained(b - 1, "proj")
                            last = nc.scalar.activation(aT[:, :, :], W[:, :].rearrange("p (c t) -> p c t", c=2), ACT.Copy)
                        elif name in ("h2T0", "h2T1"):
                            drained(b - 1, "route")
                            last = nc.scalar.activation(h2T[:, int(name[3]), :], W[:, 0:256], ACT.Copy)
                        last.then_inc(work_drained[bank], 1)
                        if name in ("q", "k"):
                            act.wait_ge(work_drained[bank], use + 1)
                            need(act, out, 16 * g)
                            nc.scalar.activation(parts[:, 0, :, 0:n], dst[:, :, 0:n], ACT.Copy).then_inc(cast, 1)

            @block.vector
            def _(dve):
                if kind == "A":
                    nc.vector.memset(best[:, :], 0.0).then_inc(reduced, 1)
                    dve.wait_ge(reduced, 1)
                if kind == "F":
                    nc.vector.memset(rstd[:, :, :], 1.0).then_inc(rstd_set, 1)
                    dve.wait_ge(rstd_set, 1)
                if kind == "X":
                    for k in KS:
                        nc.vector.memset(k[0:96, :, 120:121], 0.0)
                    nc.vector.memset(V[0][:, :, :, 0:HD], 0.0)
                    nc.vector.memset(V[1][:, :, :, 0:HD], 0.0).then_inc(zeroed, 1)
                    dve.wait_ge(zeroed, 1)
                for b, par in iterations(dve):
                    def drained(b, name):
                        if present(b, name):
                            bk, us = filling(b, name)
                            need(dve, work_drained[bk], us + 1)

                    for name, i, g, gp in steps(b, par):
                        if name in UNITS:
                            bank, use = filling(b, name)
                            W = work[bank]
                        if name in LINKS:
                            chain = Chain(dve, link_v, linked(b, name), LINKS[name], C["passed"])
                        if name == "maxima":
                            dve.wait_ge(score_full, G * g + i + 1)
                            if kind == "A":
                                src, dst = score[i % SB][:, 0:384].rearrange("p (n k) -> p n k", n=3), tops[:, 0:3, i]
                            else:
                                src = score[i % SB][:, 0:2 * HB * KN].rearrange("p (u n k) -> p u n k", u=HB, n=2)
                                dst = tops[:, 0:2, HB * i:HB * i + HB].rearrange("p n u -> p u n")
                            nc.vector.tensor_reduce(dst, src, AX.X, ALU.max).then_inc(score_read, 1)
                        if name == "top":
                            dve.wait_ge(score_read, G * g + G)
                            drained(b - 1, "rows")
                            if kind == "A":
                                nc.vector.tensor_copy(top2[:, 0, :], tops[:, 2, :])
                                chain.step(nc.vector.tensor_tensor(top2[:, 1, :], tops[:, 0, :], tops[:, 1, :], ALU.max))
                            else:
                                chain.step(nc.vector.tensor_copy(top2[:, :, :], tops[:, 0:2, :]))
                            chain.step(nc.vector.tensor_copy(top_parts[:, :, 0, :], top2[:, :, :]))
                            chain.step(nc.vector.tensor_tensor(top_parts[:, :, 1, :], top2[:, :, :], top_parts[:, :, 0, :],
                                                               ALU.subtract))
                        if name == "norm" and kind == "A":
                            dve.wait_ge(x_in, 16 * g + 16)
                            drained(b, "xT1")
                            for j in range(2):
                                last = nc.vector.tensor_scalar(grid[:, j, :], xin[:, j, :], C["xmean"][:, bass.ds(2 * g + j, 1)],
                                                               C["xrstd"][:, bass.ds(2 * g + j, 1)], ALU.subtract, ALU.mult)
                            chain.step(last)
                            chain.step(nc.vector.tensor_scalar(grid[:, :, :], grid[:, :, :], C["xinv"][:, :], MAGIC,
                                                               ALU.mult, ALU.add))
                            chain.step(nc.vector.tensor_scalar(grid[:, :, :], grid[:, :, :], MAGIC + 127.0, MAGIC - 128.0,
                                                               ALU.min, ALU.max))
                            nc.vector.tensor_scalar(xw[:, :, :], grid[:, :, :], MAGIC, None, ALU.subtract).then_inc(normed, 1)
                            chain.close()
                        if name == "norm" and kind == "X":
                            dve.wait_ge(y_in, 16 * g + 16)
                            drained(b - 1, "yT")
                            chain.step(nc.vector.tensor_scalar(grid[:, :, :], yin[:, :, :], C["yinv"][:, :], MAGIC,
                                                               ALU.mult, ALU.add))
                            chain.step(nc.vector.tensor_scalar(grid[:, :, :], grid[:, :, :], MAGIC + 127.0, MAGIC - 128.0,
                                                               ALU.min, ALU.max))
                            nc.vector.tensor_scalar(yint[:, :, :], grid[:, :, :], MAGIC, None, ALU.subtract)\
                                .then_inc(y_ready, 1)
                        if name == "wo":
                            dve.wait_ge(xb_ready, g + 1)
                            need(dve, x1_out, 16 * g)
                            dve.wait_ge(work_full[bank], use + 1)
                            nc.vector.scalar_tensor_tensor(x1[:, :, :].rearrange("p j f -> p (j f)"), W[:, :],
                                                           C["yo_scale"][:, :], xb[:, :, :].rearrange("p j f -> p (j f)"),
                                                           ALU.mult, ALU.add).then_inc(work_drained[bank], 1)
                        if name in ("stats", "ustats"):
                            if name == "ustats":
                                pb, pu = filling(b, "proj")
                                dve.wait_ge(work_drained[pb], pu + 1)
                            elif kind == "X":
                                wb, wu = filling(b, "wo")
                                dve.wait_ge(work_drained[wb], wu + 1)
                            else:
                                dve.wait_ge(x_in, 16 * g + 16)
                            x, st = (summed, ustats) if name == "ustats" else (x1 if kind == "X" else xin, stats)
                            nc.vector.bn_stats(st[:, 0, :], x[:, 0, :])
                            nc.vector.bn_stats(st[:, 1, :], x[:, 1, :]).then_inc(link_v, 1)
                        if name in ("aggr", "uaggr"):
                            st, mv = (ustats, umean_var) if name == "uaggr" else (stats, mean_var)
                            hold(dve, link_v, linked(b, name), C["passed"])
                            nc.vector.bn_aggr(mv[:, 0, :], st[:, 0, :])
                            nc.vector.bn_aggr(mv[:, 1, :], st[:, 1, :]).then_inc(link_v, 1)
                        if name in ("var", "uvar"):
                            mv, at = (umean_var, 4) if name == "uvar" else (mean_var, 0)
                            dve.wait_ge(link_v, linked(b, name))
                            if name == "var" and kind == "F":
                                nc.vector.tensor_scalar(rstd[:, 0, 2:4], mv[:, :, 1], 1.0 + 1e-5, 1e-10, ALU.mult, ALU.add)
                            nc.vector.tensor_scalar(rstd[:, 0, at:at + 2], mv[:, :, 1], 1e-5, None, ALU.add).then_inc(link_v, 1)
                        if name in NEWTON_OPS:
                            dve.wait_ge(link_v, linked(b, name))
                            inverse_root(nc, int(name[1:]), rstd[:, 0, :], rstd[:, 1, :], rstd[:, 2, :]).then_inc(link_v, 1)
                        if name == "apply":
                            dve.wait_ge(link_v, linked(b, NEWTON_OPS[-1]) + 1)
                            drained(b, "xT")
                            if kind == "F":
                                need(dve, z_out, 16 * g)
                            x = x1 if kind == "X" else xin
                            for j in range(2):
                                if kind == "F":
                                    nc.vector.tensor_scalar(z[:, j, :], x[:, j, :], mean_var[:, j, 0:1], rstd[:, 1, j:j + 1],
                                                            ALU.subtract, ALU.mult)
                                at = j + 2 if kind == "F" else j
                                last = nc.vector.tensor_scalar(xw[:, j, :], x[:, j, :], mean_var[:, j, 0:1],
                                                               rstd[:, 1, at:at + 1], ALU.subtract, ALU.mult)
                            last.then_inc(normed, 1)
                        if name == "uapply":
                            dve.wait_ge(link_v, linked(b, NEWTON_OPS[-1]) + 1)
                            need(dve, h2_ready, 2 * g)
                            for j in range(2):
                                last = nc.vector.tensor_scalar(hn[:, j, :], summed[:, j, :], umean_var[:, j, 0:1],
                                                               rstd[:, 1, 4 + j:5 + j], ALU.subtract, ALU.mult)
                            last.then_inc(hn_ready, 1)
                        if name == "v":
                            dve.wait_ge(work_full[bank], use + 1)
                            need(dve, pv_done, 4 * (g - 1))
                            n, r = (16, 120) if kind == "X" else (32, P)
                            dst = V[gp][0:r, 0:n // 16, :, 0:HD].rearrange("p a h d -> p (a h) d")
                            src = W[0:r, 0:n * HD].rearrange("p (a d) -> p a d", d=HD)
                            if kind == "X":
                                last = nc.vector.tensor_copy(dst, src)
                            else:
                                scale = C["qkv_scale"][:, 2:3] if kind == "A" else 1.0
                                bias = C["bv" + kind][:, :].rearrange("p (a d) -> p a d", d=HD)
                                last = nc.vector.scalar_tensor_tensor(dst, src, scale, bias, ALU.mult, ALU.add)
                            last.then_inc(work_drained[bank], 1)
                        if name in ("tok0", "tok1"):
                            j = int(name[3])
                            dve.wait_ge(work_full[bank], use + 1)
                            if kind == "A" and j == 0:
                                need(dve, result_out, 16 * g)
                            elif j == 0:
                                drained(b - 1, "aT")
                            v = W[:, :].rearrange("p (h d) -> p h d", d=VW)
                            chain.step(nc.vector.reciprocal(rec[:, j, :], v[:, :, HD]))
                            nc.vector.tensor_tensor(tok[:, j, :].rearrange("p (h d) -> p h d", d=HD), v[:, :, 0:HD],
                                                    rec[:, j, :].unsqueeze(2).broadcast_to([P, H, HD]), ALU.mult)\
                                .then_inc(work_drained[bank], 1)
                            if kind == "A" and j == 1:
                                dve.wait_ge(work_drained[bank], use + 1)
                                chain.step(nc.vector.tensor_reduce(absmax[:, :], tok[:, :, :], AX.XY, ALU.max,
                                                                   apply_absolute_value=True))
                                chain.step(nc.vector.tensor_tensor(best[:, :], best[:, :], absmax[:, :], ALU.max))
                        if name == "proj":
                            dve.wait_ge(work_full[bank], use + 1)
                            dve.wait_ge(based_ready, g + 1)
                            if kind == "X":
                                need(dve, result_out, 16 * g)
                            else:
                                need(dve, xu_ready, g)
                            nc.vector.tensor_tensor(summed[:, :, :].rearrange("p j f -> p (j f)"), W[:, :],
                                                    based[:, :, :].rearrange("p j f -> p (j f)"), ALU.add)\
                                .then_inc(work_drained[bank], 1)
                        if name == "route":
                            dve.wait_ge(work_full[bank], use + 1)
                            nc.vector.tensor_copy(C["logits"][:, bass.ds(2 * g, 2), :],
                                                  W[:, 0:16].rearrange("p (j e) -> p j e", e=8))\
                                .then_inc(work_drained[bank], 1)
                if kind == "A":
                    dve.wait_ge(reduced, 2)
                    nc.vector.tensor_scalar(C["yscale"][:, :], best_all[:, :], 1.0 / 127.0, 1e-8, ALU.mult, ALU.max)\
                        .then_inc(reduced, 1)
                    dve.wait_ge(reduced, 3)
                    nc.vector.reciprocal(C["yinv"][:, :], C["yscale"][:, :]).then_inc(reduced, 1)
                    nc.vector.tensor_tensor(C["yo_scale"][:, :], C["yscale"][:, :], C["wscale"][:, 3:4], ALU.mult)\
                        .then_inc(reduced, 1)
                    dve.wait_ge(reduced, 5)

            @block.gpsimd
            def _(pool):
                if kind == "X":
                    for m in mask:
                        nc.gpsimd.memset(m[:, :, :], 0.0).then_inc(mask_zero, 1)
                    pool.wait_ge(mask_zero, 2)
                for b, par in iterations(pool):
                    for name, i, g, gp in steps(b, par):
                        def drained(b, name):
                            if present(b, name):
                                bk, us = filling(b, name)
                                need(pool, work_drained[bk], us + 1)

                        if name in ("q", "k"):
                            src, parts, cast, rest, n = (q_f, q_parts, q_cast0, q_rest, 256) if name == "q" else \
                                (k_f, k_parts, k_cast0, k_rest, KT)
                            pool.wait_ge(cast, g + 1)
                            nc.gpsimd.tensor_tensor(left[:, :, 0:n], src[:, :, 0:n], parts[:, 0, :, 0:n], ALU.subtract)\
                                .then_inc(rest, 1)
                        if name in ("q_rest", "k_rest"):
                            parts, cast, split, n = (q_parts, q_cast1, q_split, 256) if name[0] == "q" else \
                                (k_parts, k_cast1, k_split, KT)
                            pool.wait_ge(cast, g + 1)
                            nc.gpsimd.tensor_tensor(parts[:, 2, :, 0:n], left[:, :, 0:n], parts[:, 1, :, 0:n], ALU.subtract)\
                                .then_inc(split, 1)
                            pool.wait_ge(split, g + 1)
                        if name == "fetch" and kind == "X":
                            pool.wait_ge(x_in, 16 * g + 16)
                            drained(b - 1, "wo")
                            nc.gpsimd.tensor_tensor(xb[:, :, :], xin[:, :, :], C["bo_a"][:, :, :], ALU.add).then_inc(xb_ready, 1)
                        if name == "load" and kind == "X":
                            pool.wait_ge(mask_in, 16 * g + 16)
                            hold(pool, scoreT_full, G * (g - 1), C["passed"])
                            nc.gpsimd.tensor_scalar(mask[gp][:, :, 0:120], mraw[:, :, :], MASKED, None, ALU.mult)\
                                .then_inc(mask_ready, 1)
                        if name == "refetch" and kind == "X":
                            pool.wait_ge(xres_in, 16 * g + 16)
                            drained(b - 1, "proj")
                            nc.gpsimd.tensor_tensor(based[:, :, :], xres[:, :, :], C["bproj"][:, :, :], ALU.add)\
                                .then_inc(based_ready, 1)
                        if name == "refetch" and kind == "F":
                            pool.wait_ge(zres_in, 16 * g + 16)
                            drained(b - 1, "proj")
                            nc.gpsimd.tensor_tensor(based[:, :, :], zres[:, :, :], C["bo_f"][:, :, :], ALU.add)\
                                .then_inc(based_ready, 1)
                        if name == "uapply":
                            drained(b, "proj")
                            pool.wait_ge(xres_in, 16 * g + 16)
                            need(pool, result_out, 16 * g)
                            nc.gpsimd.tensor_tensor(xu[:, :, :], summed[:, :, :], xres[:, :, :], ALU.add).then_inc(xu_ready, 1)
                            pool.wait_ge(hn_ready, g + 1)
                            need(pool, h2_out, 16 * g)
                            drained(b, "h2T1")
                            nc.gpsimd.tensor_tensor(h2[:, :, :], hn[:, :, :], C["ln2_g"][:, :, :], ALU.mult)\
                                .then_inc(h2_ready, 1)
                            pool.wait_ge(h2_ready, 2 * g + 1)
                            nc.gpsimd.tensor_tensor(h2[:, :, :], h2[:, :, :], C["ln2_b"][:, :, :], ALU.add)\
                                .then_inc(h2_ready, 1)
                            pool.wait_ge(h2_ready, 2 * g + 2)
                if kind == "A":
                    pool.wait_ge(link_v, linked(LAST + 1, ORDER[0]))
                    nc.gpsimd.partition_all_reduce(best_all[:, :], best[:, :], P, bass.bass_isa.ReduceOp.max)\
                        .then_inc(reduced, 1)
                    pool.wait_ge(reduced, 2)



NE = 8
ROW = 258


def route(nc, C, D, io):
    NT, CAP = D["T"] // P, D["CAP"]
    with ExitStack() as ctx:
        sb, ps, sem = allocators(nc, ctx, "route_")
        L = C["logits"]
        first, hit, other, spread = (sb(n, [P, NT, NE]) for n in ("first", "hit", "other", "spread"))
        one = [sb(f"one{i}", [P, NT, NE]) for i in range(2)]
        one_b = [sb(f"one_b{i}", [P, NT, NE], BF16) for i in range(2)]
        loc = sb("loc", [P, NT, NE])
        run = [sb(f"run{i}", [P, NT, NE]) for i in range(2)]
        down, ones = sb("down", [P, NE]), sb("ones", [P, NT])
        top = [sb(f"top{i}", [P, NT]) for i in range(2)]
        rank = [sb(f"rank{i}", [P, NT]) for i in range(2)]
        pos = [sb(f"pos{i}", [P, NT]) for i in range(2)]
        kept = [sb(f"kept{i}", [P, NT]) for i in range(2)]
        prob = [sb(f"prob{i}", [P, NT]) for i in range(2)]
        base, slot, total, den = sb("base", [P, NT]), sb("slot", [P, NT]), sb("total", [P, NT]), sb("den", [P, NT])
        b1_rows = sb("b1_rows", [NE * 8, P])
        HALF = max(NT * NE // 512, 1)
        W = NT * NE // HALF
        inside = [ps(f"inside{i}", [P, HALF, 512]) for i in range(2)]
        whole = [ps(f"whole{i}", [P, HALF, 512]) for i in range(2)]
        link, hot, counted, spread_in, exped, b1_in, b1_turned = (
            sem(n) for n in ("link", "hot", "counted", "spread_in", "exped", "b1_in", "b1_turned"))

        def flat(t):
            return t[:, :, :].rearrange("p n e -> p (n e)")

        def cols(t):
            return t[:, :, 0:W] if HALF > 1 else t[:, 0, 0:W]

        def halves(t):
            return flat(t).rearrange("p (a w) -> p a w", a=HALF) if HALF > 1 else flat(t)

        def wide(t):
            return t[:, :].unsqueeze(2).broadcast_to([P, NT, NE])

        with nc.Block() as block:
            @block.sync
            def _(sp):
                sp.dma_start(b1_rows[:, :], io["L0_ffn_b1"].rearrange("e (f p) -> (e f) p", p=P)).then_inc(b1_in, 16)

            @block.tensor
            def _(pe):
                for i in range(2):
                    pe.wait_ge(hot, i + 1)
                    for a in range(HALF):
                        m = flat(one_b[i])[:, a * W:(a + 1) * W]
                        nc.tensor.matmul(inside[i][:, a, 0:W], C["below"][:, :], m, start=True, stop=True)
                        last = nc.tensor.matmul(whole[i][:, a, 0:W], C["ones_b"][:, :], m, start=True, stop=True)
                    last.then_inc(counted, 1)
                pe.wait_ge(counted, 3)
                pe.wait_ge(b1_in, 16)
                nc.tensor.transpose(inside[0][:, 0, 0:NE * 8], b1_rows[:, :], C["ident_f"][0:NE * 8, 0:NE * 8])\
                    .then_inc(b1_turned, 1)

            @block.scalar
            def _(act):
                act.wait_ge(spread_in, 1)
                nc.scalar.activation(flat(other), flat(spread), ACT.Exp)
                nc.scalar.activation(prob[1][:, :], total[:, :], ACT.Exp).then_inc(exped, 1)

            @block.vector
            def _(dve):
                chain = Chain(dve, link, 0, None, C["passed"])
                v = nc.vector
                for e in range(NE):
                    v.memset(down[:, e:e + 1], float(NE - e))
                v.memset(ones[:, :], 1.0)
                chain.step(v.tensor_copy(flat(first), flat(L)))
                down3 = down[:, :].unsqueeze(1).broadcast_to([P, NT, NE])
                for i in range(2):
                    chain.step(v.tensor_reduce(top[i][:, :], first[:, :, :], AX.X, ALU.max))
                    chain.step(v.tensor_tensor(hit[:, :, :], first[:, :, :], wide(top[i]), ALU.is_equal))
                    chain.step(v.tensor_tensor(hit[:, :, :], hit[:, :, :], down3, ALU.mult))
                    chain.step(v.tensor_reduce(rank[i][:, :], hit[:, :, :], AX.X, ALU.max))
                    chain.step(v.tensor_tensor(one[i][:, :, :], wide(rank[i]), down3, ALU.is_equal))
                    v.tensor_copy(flat(one_b[i]), flat(one[i])).then_inc(hot, 1)
                    if i == 0:
                        chain.step(v.scalar_tensor_tensor(flat(first), flat(one[0]), -3e38, flat(first), ALU.mult, ALU.add))
                v.tensor_tensor(spread[:, :, :], L[:, :, :], wide(top[0]), ALU.subtract)
                v.tensor_tensor(total[:, :], top[1][:, :], top[0][:, :], ALU.subtract).then_inc(spread_in, 1)
                dve.wait_ge(exped, 1)
                chain.step(v.tensor_reduce(den[:, :], other[:, :, :], AX.X, ALU.add))
                chain.step(v.reciprocal(prob[0][:, :], den[:, :]))
                chain.step(v.tensor_tensor(prob[1][:, :], prob[1][:, :], prob[0][:, :], ALU.mult))
                for i in range(2):
                    dve.wait_ge(counted, i + 1)
                    chain.step(v.tensor_copy(halves(hit), cols(whole[i])))
                    for e in range(NE):
                        last = v.tensor_tensor_scan(run[i][:, :, e], ones[:, :], hit[:, :, e], 0.0, ALU.mult, ALU.add)
                    chain.step(last)
                    chain.step(v.tensor_tensor(flat(loc), flat(run[i]), flat(hit), ALU.subtract))
                    chain.step(v.tensor_tensor(halves(loc), cols(inside[i]), halves(loc), ALU.add))
                    if i == 1:
                        every = run[0][:, NT - 1:NT, :].broadcast_to([P, NT, NE])
                        chain.step(v.tensor_tensor(loc[:, :, :], loc[:, :, :], every, ALU.add))
                    chain.step(v.tensor_tensor(flat(loc), flat(loc), flat(one[i]), ALU.mult))
                    chain.step(v.tensor_reduce(pos[i][:, :], loc[:, :, :], AX.X, ALU.add))
                    chain.step(v.tensor_scalar(pos[i][:, :], pos[i][:, :], -1.0, None, ALU.add))
                    chain.step(v.tensor_scalar(kept[i][:, :], pos[i][:, :], float(CAP), None, ALU.is_lt))
                    chain.step(v.tensor_scalar(base[:, :], rank[i][:, :], -float(CAP), float(NE * CAP), ALU.mult, ALU.add))
                    chain.step(v.tensor_tensor(slot[:, :], pos[i][:, :], base[:, :], ALU.add))
                    chain.step(v.tensor_scalar(base[:, :], kept[i][:, :], -float(4 * NE * CAP), float(4 * NE * CAP),
                                               ALU.mult, ALU.add))
                    chain.step(v.tensor_tensor(slot[:, :], slot[:, :], base[:, :], ALU.add))
                    chain.step(v.tensor_copy(C["scatter"][i][:, :], slot[:, :]))
                    chain.step(v.tensor_tensor(prob[i][:, :], prob[i][:, :], kept[i][:, :], ALU.mult))
                chain.step(v.tensor_tensor(den[:, :], prob[0][:, :], prob[1][:, :], ALU.add))
                chain.step(v.tensor_scalar(den[:, :], den[:, :], 1.1920928955078125e-07, None, ALU.max))
                chain.step(v.reciprocal(total[:, :], den[:, :]))
                for i in range(2):
                    chain.step(v.tensor_tensor(base[:, :], prob[i][:, :], total[:, :], ALU.mult))
                    chain.step(v.tensor_tensor(C["gate"][i][:, :], base[:, :], kept[i][:, :], ALU.mult))
                v.memset(ones[:, 0:1], 0.0).then_inc(counted, 1)
                dve.wait_ge(b1_turned, 1)
                chain.step(v.tensor_copy(C["b1"][:, :], inside[0][:, 0, 0:NE * 8]))



def dispatch(nc, C, D, io, scratch):
    NT, CAP = D["T"] // P, D["CAP"]
    R = 4
    with ExitStack() as ctx:
        sb, ps, sem = allocators(nc, ctx, "disp_")
        row = [[sb(f"row{i}_{k}", [P, ROW]) for k in range(R)] for i in range(2)]
        index = [[sb(f"index{i}_{k}", [P, 1], I32) for k in range(R)] for i in range(2)]
        h2_in, sent = [[[sem(f"{n}{i}_{k}") for k in range(R)] for i in range(2)] for n in ("h2_in", "sent")]
        tail_ready = sem("tail_ready")
        with nc.Block() as block:
            @block.sync
            def _(sp):
                for r in rounds(sp, NT // R):
                    for k in range(R):
                        for i in range(2):
                            need(sp, sent[i][k], 16 * r)
                            sp.dma_start(row[i][k][:, 0:256], scratch["h2"][bass.ds((R * r + k) * P, P), :])\
                                .then_inc(h2_in[i][k], 16)

            @block.vector
            def _(dve):
                for r in rounds(dve, NT // R):
                    for k in range(R):
                        for i in range(2):
                            need(dve, sent[i][k], 16 * r)
                            n = bass.ds(R * r + k, 1)
                            nc.vector.tensor_copy(index[i][k][:, :], C["scatter"][i][:, n])
                            nc.vector.tensor_copy(row[i][k][:, 256:257].bitcast(I32), C["number"][:, n])
                            nc.vector.tensor_copy(row[i][k][:, 257:258], C["gate"][i][:, n]).then_inc(tail_ready, 1)

            @block.gpsimd
            def _(pool):
                pool.wait_ge(C["slots_cleared"], 16 * D["B"])
                for r in rounds(pool, NT // R):
                    for k in range(R):
                        for i in range(2):
                            hold(pool, tail_ready, 2 * (R * r + k) + i + 1, C["passed"])
                            hold(pool, h2_in[i][k], 16 * r + 16, C["passed"])
                            nc.gpsimd.indirect_dma_start(
                                scratch["slots"], bass.IndirectOffsetOnAxis(index[i][k][:, 0:1], 0), row[i][k][:, :], None,
                                bounds_check=NE * CAP - 1, oob_is_err=False).then_inc(sent[i][k], 16)
                for k in range(R):
                    for i in range(2):
                        pool.wait_ge(sent[i][k], 16 * (NT // R))



def experts(nc, C, D, io, scratch, out):
    CAP = D["CAP"]
    NS = 512
    NC = CAP // NS
    NF = 1024 // P
    with ExitStack() as ctx:
        sb, ps, sem = allocators(nc, ctx, "exp_")
        w1 = [sb(f"w1{i}", [P, 2, 1024]) for i in range(2)]
        w2 = [sb(f"w2{i}", [P, NF, 256]) for i in range(2)]
        b1 = [sb(f"b1{i}", [P, NF]) for i in range(2)]
        b2 = [sb(f"b2{i}", [P, 256]) for i in range(2)]
        b2s = [sb(f"b2s{i}", [P, 2, 256]) for i in range(2)]
        x = [sb(f"x{i}", [P, 4, ROW]) for i in range(2)]
        xT = [sb(f"xT{i}", [P, 2, NS]) for i in range(2)]
        hT = [sb(f"hT{i}", [P, NF, NS]) for i in range(2)]
        y = [sb(f"y{i}", [P, 4, 256]) for i in range(2)]
        gated = [sb(f"gated{i}", [P, 4, 256]) for i in range(2)]
        turn = [ps(f"turn{i}", [P, NS]) for i in range(2)]
        hid = [ps(f"hid{i}", [P, NS]) for i in range(2)]
        res = [ps(f"res{i}", [P, 2, 256]) for i in range(2)]
        w_in = [sem(f"w_in{i}") for i in range(2)]
        x_in = [sem(f"x_in{i}") for i in range(2)]
        (turned, xT_ready, hid_full, hid_read, res_full, res_read, biases, gated_ready, added) = (sem(n) for n in (
            "turned", "xT_ready", "hid_full", "hid_read", "res_full", "res_read", "biases", "gated_ready", "added"))

        def ends_apart(eng):
            for r in rounds(eng, NE // 2 - 1):
                yield r
            yield NE // 2 - 1

        def another(n):
            return not isinstance(n, int) or n + 1 < NE * NC

        def chunks(r):
            for k in range(2):
                for c in range(NC):
                    j = k * NC + c
                    yield 2 * r + k, k, c, j % 2, 2 * NC * r + j

        with nc.Block() as block:
            @block.sync
            def _(sp):
                def weights(e, k):
                    for dst, src in ((w1[k][:, :, :], io["L0_ffn_w1"][bass.ds(e * 256, 256), :].rearrange("(c p) f -> p c f", p=P)),
                                     (w2[k][:, :, :], io["L0_ffn_w2"][bass.ds(e * 1024, 1024), :].rearrange("(f p) n -> p f n", p=P)),
                                     (b2[k][:, :], io["L0_ffn_b2"][bass.ds(e, 1), :].partition_broadcast(P))):
                        sp.dma_start(dst, src).then_inc(w_in[k], 16)

                def rows_in(k, n):
                    sp.dma_start(x[k][:, :, :], scratch["slots"][bass.ds(n * NS, NS), :].rearrange("(j p) f -> p j f", p=P))\
                        .then_inc(x_in[k], 16)

                weights(0, 0)
                rows_in(0, 0)
                weights(1, 1)

                for r in ends_apart(sp):
                    for e, k, c, par, n in chunks(r):
                        if another(n):
                            hold(sp, added, 64 * n, C["passed"])
                            rows_in(1 - par, n + 1)
                        if c == NC - 1 and not (isinstance(r, int) and r == NE // 2 - 1):
                            sp.wait_ge(res_read, 2 * n + 2)
                            weights(e + 2, k)

                for k in range(2):
                    sp.wait_ge(w_in[k], 48 * (NE // 2))

            @block.tensor
            def _(pe):
                def turn_rows(n, par):
                    pe.wait_ge(x_in[par], 8 * (n - par) + 16)
                    need(pe, xT_ready, 2 * n)
                    for a in range(2):
                        for j in range(4):
                            last = nc.tensor.transpose(turn[a][:, j * P:(j + 1) * P], x[par][:, j, a * P:(a + 1) * P],
                                                       C["ident_f"][:, :])
                        last.then_inc(turned, 1)

                turn_rows(0, 0)
                for r in ends_apart(pe):
                    for e, k, c, par, n in chunks(r):
                        if c == 0:
                            pe.wait_ge(w_in[k], 48 * r + 48)
                        pe.wait_ge(xT_ready, 2 * n + 2)
                        for f in range(NF):
                            m = NF * n + f
                            if k or c or f >= 2:
                                need(pe, hid_read, m - 1)
                            h = hid[f % 2]
                            for a in range(2):
                                last = nc.tensor.matmul(h[:, :], w1[k][:, a, f * P:(f + 1) * P], xT[par][:, a, :],
                                                        start=a == 0, stop=a == 1)
                            last.then_inc(hid_full, 1)
                        if another(n):
                            turn_rows(n + 1, 1 - par)
                        pe.wait_ge(hid_read, NF * n + NF)
                        for t in range(2):
                            need(pe, res_read, 2 * n)
                            for s in range(2):
                                for f in range(NF):
                                    last = nc.tensor.matmul(res[t][:, s, :], hT[par][:, f, (2 * t + s) * P:(2 * t + s + 1) * P],
                                                            w2[k][:, f, :], start=f == 0, stop=f == NF - 1)
                            last.then_inc(res_full, 1)

            @block.scalar
            def _(act):
                for r in rounds(act, NE // 2):
                    for e, k, c, par, n in chunks(r):
                        if c == 0:
                            act.wait_ge(biases, 2 * e + 2)
                        for f in range(NF):
                            act.wait_ge(hid_full, NF * n + f + 1)
                            nc.scalar.activation(hT[par][:, f, :], hid[f % 2][:, :], ACT.Relu, bias=b1[k][:, f:f + 1])\
                                .then_inc(hid_read, 1)

            @block.vector
            def _(dve):
                def copy_rows(n, par):
                    for a in range(2):
                        dve.wait_ge(turned, 2 * n + a + 1)
                        nc.vector.tensor_copy(xT[par][:, a, :], turn[a][:, :]).then_inc(xT_ready, 1)

                copy_rows(0, 0)
                for r in ends_apart(dve):
                    for e, k, c, par, n in chunks(r):
                        if c == 0:
                            dve.wait_ge(w_in[k], 48 * r + 48)
                            nc.vector.tensor_copy(b1[k][:, :], C["b1"][:, bass.ds(e * NF, NF)]).then_inc(biases, 1)
                            for s in range(2):
                                last = nc.vector.tensor_scalar(b2s[k][:, s, :], b2[k][:, :], 0.8, None, ALU.mult)
                            last.then_inc(biases, 1)
                            dve.wait_ge(biases, 2 * e + 2)
                        if another(n):
                            copy_rows(n + 1, 1 - par)
                        for t in range(2):
                            dve.wait_ge(res_full, 2 * n + t + 1)
                            nc.vector.scalar_tensor_tensor(
                                y[par][:, 2 * t:2 * t + 2, :].rearrange("p s n -> p (s n)"),
                                res[t][:, :, :].rearrange("p s n -> p (s n)"), 0.8,
                                b2s[k][:, :, :].rearrange("p s n -> p (s n)"), ALU.mult, ALU.add).then_inc(res_read, 1)
                            dve.wait_ge(res_read, 2 * n + t + 1)
                            if t == 0:
                                need(dve, added, 64 * (n - 1))
                            for s in (2 * t, 2 * t + 1):
                                last = nc.vector.tensor_scalar(gated[par][:, s, :], y[par][:, s, :], x[par][:, s, 257:258],
                                                               None, ALU.mult)
                            last.then_inc(gated_ready, 1)

            @block.gpsimd
            def _(pool):
                for r in rounds(pool, NE // 2):
                    for e, k, c, par, n in chunks(r):
                        for t in range(2):
                            hold(pool, gated_ready, 2 * n + t + 1, C["passed"])
                            for s in (2 * t, 2 * t + 1):
                                hold(pool, added, 64 * n + 16 * s, C["passed"])
                                nc.gpsimd.indirect_dma_start(
                                    out, bass.IndirectOffsetOnAxis(x[par][:, s, 256:257].bitcast(I32), 0),
                                    gated[par][:, s, :], None, bounds_check=D["T"] - 1, oob_is_err=False,
                                    compute_op=ALU.add).then_inc(added, 16)
                pool.wait_ge(added, 64 * NE * NC)



def program(nc, io, out):
    B = io["x"].shape[0] // 256
    T = B * 256
    CAP = -(-T // 4)
    D = {"B": B, "T": T, "CAP": CAP, "CLEARED": NE * CAP // B}
    ctx = ExitStack()
    with ctx:
        sb, ps, sem = allocators(nc, ctx, "")

        def dram(name, shape, dtype=F32):
            return nc.dram_tensor(name, shape, dtype).ap()

        scratch = {n: dram("d_" + n, [T, 256]) for n in ("y", "x1", "x2", "z", "h2")}
        for name, tokens in (("q", 256), ("k", 256), ("k120", 120)):
            scratch[name] = dram("d_" + name, [3, HD, H * tokens], BF16)
        scratch["slots"], scratch["out"] = dram("d_slots", [NE * CAP, ROW]), out
        C = {
            "slots_cleared": sem("slots_cleared"), "passed": sem("passed"), "b1": sb("b1", [P, NE * 8]),
            "number": sb("number", [P, 2 * B], I32), "empty": sb("empty", [P, 4, ROW]),
            "scatter": [sb(f"scatter{i}", [P, 2 * B], I32) for i in range(2)],
            "gate": [sb(f"gate{i}", [P, 2 * B]) for i in range(2)],
            "ident_f": sb("ident_f", [P, P]), "ident_b": sb("ident_b", [P, P], BF16),
            "causal": sb("causal", [P, 2 * P], BF16), "below": sb("below", [P, P], BF16),
            "ones_b": sb("ones_b", [P, P], BF16), "wscale": sb("wscale", [P, 4]), "wT": sb("wT", [P, 4, 2, 256], BF16),
            "QS": [sb(f"QS{i}", [98, H, 256], BF16) for i in range(2)],
            "KS": [sb(f"KS{i}", [98, H, 256], BF16) for i in range(2)],
            "V": [sb(f"V{i}", [P, 2, H, VW]) for i in range(2)], "xmean": sb("xmean", [P, 2 * B]), "xrstd": sb("xrstd", [P, 2 * B]),
            "xscale": sb("xscale", [P, 1]), "qkv_scale": sb("qkv_scale", [P, 3]), "yscale": sb("yscale", [P, 1]),
            "xinv": sb("xinv", [P, 1]), "yinv": sb("yinv", [P, 1]),
            "yo_scale": sb("yo_scale", [P, 1]), "logits": sb("logits", [P, 2 * B, 8]),
        }
        C["columns"] = [("L0_ffn_ln1_g", "ln1_g"), ("L0_ffn_ln1_b", "ln1_b")]
        C["biases"] = [("L0_attn_bq", "bq_a"), ("L0_attn_bk", "bk_a"), ("L0_ffn_bq", "bq_f"), ("L0_ffn_bk", "bk_f")]
        C["broadcasts"] = [("L0_attn_bv", "bvA"), ("L0_ffn_bv", "bvF"), ("L0_attn_bo", "bo_a"), ("L0_xattn_bproj", "bproj"),
                           ("L0_ffn_bo", "bo_f"), ("L0_ffn_ln2_g", "ln2_g"), ("L0_ffn_ln2_b", "ln2_b")]
        C["ordered"] = [("L0_xattn_Wq", "xq"), ("L0_xattn_Wkv", "xk"), ("L0_ffn_wq", "fq"), ("L0_ffn_wk", "fk")]
        for name, key in C["ordered"]:
            C[key] = sb("w_" + key, [P, 2, 256])
        C["matrices"] = [("L0_xattn_Wkv", "xv", 256), ("L0_xattn_Wproj", "xo", 256),
                         ("L0_ffn_wv", "fv", 256),
                         ("L0_ffn_wo", "fo", 256), ("L0_ffn_wr", "wr", 8)]
        for name, key in C["columns"] + C["biases"]:
            C[key] = sb(key, [P, 2])
        for name, key in C["broadcasts"]:
            C[key] = sb(key, [P, 2, 256]) if key[:2] != "bv" else sb(key, [P, 512])
        for name, key, n in C["matrices"]:
            C[key] = sb("w_" + key, [P, 2, n])
        C["columns"] = [(n, C[k][:, :]) for n, k in C["columns"]]
        C["biases"] = [(n, C[k][:, :]) for n, k in C["biases"]]
        C["broadcasts"] = [(n, C[k][:, j, :] if k[:2] != "bv" else C[k][:, j * 256:(j + 1) * 256])
                           for n, k in C["broadcasts"] for j in range(2)]
        C["matrices"] = [(n, C[k][:, :, :]) for n, k, _ in C["matrices"]]
        C["wA"] = [C["wT"][:, i, :, :] for i in range(3)] + [None]
        C["wX"] = [C["xq"], C["xk"], C["xv"], C["xo"]]
        C["wF"] = [C["fq"], C["fk"], C["fv"], C["fo"]]
        setup(nc, C, D, io)
        first_norm(nc, C, D, io)
        attention(nc, C, D, io, scratch, "A")
        attention(nc, C, D, io, scratch, "X")
        attention(nc, C, D, io, scratch, "F")
        route(nc, C, D, io)
        dispatch(nc, C, D, io, scratch)
        experts(nc, C, D, io, scratch, out)
def layout(inputs):
    import numpy as _np
    arrays = {}
    for name, a in inputs.items():
        a = _np.ascontiguousarray(a)
        if name == "x":
            a = a.reshape(-1, 256)
        if name == "ctx_1024":
            name, a = "ctx", a.reshape(-1, 256)
        if name == "mask_BxSxS2_bk0":
            name, a = "mask", a.reshape(-1, 120)
        if name in ("L0_ffn_w1", "L0_ffn_w2"):
            a = a.reshape(-1, a.shape[-1])
        arrays[name] = a
    return arrays



def kernel(**inputs):
    import concourse.bacc as bacc
    from concourse.bass_utils import run_bass_kernel_spmd

    shape = inputs["x"].shape
    nc = bacc.Bacc("TRN2", target_bir_lowering=False, num_devices=1)
    arrays, io = {}, {}
    for name, a in layout(inputs).items():
        arrays[f"in_{name}_dram"] = a
        io[name] = nc.dram_tensor(f"in_{name}_dram", a.shape, mybir.dt.from_np(a.dtype), kind="ExternalInput").ap()
    out = nc.dram_tensor("out_dram", [shape[0] * shape[1], shape[2]], F32, kind="ExternalOutput").ap()
    program(nc, io, out)
    result = run_bass_kernel_spmd(nc, [arrays], core_ids=[0])
    return result.results[0]["out_dram"].reshape(shape)
```
